# Optimizing a Trainium2 kernel written in Bass

```python
import numpy as np
import jax
import jax.numpy as jnp

def _softmax(x, axis=-1):
    return jax.nn.softmax(x, axis=axis)

def _gelu(x):
    return jax.nn.gelu(x, approximate=True)

def _silu(x):
    return jax.nn.silu(x)

def _sigmoid(x):
    return jax.nn.sigmoid(x)

def _layernorm(x, axis=-1, eps=1e-05):
    m = jnp.mean(x, axis=axis, keepdims=True)
    v = jnp.var(x, axis=axis, keepdims=True)
    return (x - m) / jnp.sqrt(v + eps)

def _scatter_add(tgt, idx, src, axis=0):
    return tgt.at[idx].add(src)

def _segment_sum(src, seg, n):
    return jax.ops.segment_sum(src, seg, n)
kernel_name = 'mk_adj_seq_d2_adj_r2_f89641'

def setup_inputs(seed: int=0):
    np.random.seed(seed)
    _w = jnp.asarray

    def _rec_inputs():
        import jax
        import jax.numpy as jnp
        _gk = jax.random.key(seed)
        x = -0.0005207 + 1.001 * jax.random.normal(jax.random.fold_in(_gk, 1), (128, 128, 256), jnp.float32)
        _a = jax.random.bernoulli(jax.random.fold_in(_gk, 2), 0.0625, (128, 128, 128))
        _a = jnp.logical_or(_a, jnp.swapaxes(_a, -1, -2))
        _a = jnp.logical_or(_a, jnp.eye(128, dtype=bool))
        adj = _a.astype(jnp.int32)
        return (x, adj)
    x, adj = _rec_inputs()

    def _L0_gnn_setup():
        import jax, jax.numpy as jnp
        import numpy as np
        B, S, D, H = (2, 1024, 256, 8)
        HD = D // H
        EPS = 1e-05

        def _ln(x, g, b):
            mu = jnp.mean(x, axis=-1, keepdims=True)
            var = jnp.mean((x - mu) ** 2, axis=-1, keepdims=True)
            return (x - mu) * jax.lax.rsqrt(var + EPS) * g + b
        key = jax.random.key(seed)
        ks = jax.random.split(key, 16)
        x = jax.random.normal(ks[0], (B, S, D), dtype=jnp.float32)
        adj = jax.random.randint(ks[1], (B, S, S), 0, 2, dtype=jnp.int32)
        adj = adj.at[:, jnp.arange(S), jnp.arange(S)].set(1)
        edge_attr = jax.random.normal(ks[2], (B, S, S), dtype=jnp.float32)
        sc = 1.0 / np.sqrt(D)
        p = lambda k, shp: jax.random.normal(k, shp, dtype=jnp.float32) * sc
        return {'x': x, 'adj_matrix': adj, 'edge_attr_matrix': edge_attr, 'ln1_g': jnp.ones((D,)), 'ln1_b': jnp.zeros((D,)), 'ln2_g': jnp.ones((D,)), 'ln2_b': jnp.zeros((D,)), 'wq': p(ks[3], (D, D)), 'bq': jnp.zeros((D,)), 'wk': p(ks[4], (D, D)), 'bk': jnp.zeros((D,)), 'wv': p(ks[5], (D, D)), 'bv': jnp.zeros((D,)), 'wo': p(ks[6], (D, D)), 'bo': jnp.zeros((D,)), 'w1': p(ks[7], (D, 4 * D)), 'b1': jnp.zeros((4 * D,)), 'w2': p(ks[8], (4 * D, D)), 'b2': jnp.zeros((D,))}
    _L0_gnn_all = _L0_gnn_setup()
    _L0_gnn_in = {k: v for k, v in _L0_gnn_all.items() if k in ('ln1_g', 'ln1_b', 'ln2_g', 'ln2_b', 'wq', 'bq', 'wk', 'bk', 'wv', 'bv', 'wo', 'bo', 'w1', 'b1', 'w2', 'b2')}
    del _L0_gnn_all

    def _L1_gnn_setup():
        import jax, jax.numpy as jnp
        import numpy as np
        B, N, D, H = (4, 1024, 256, 8)
        HD = D // H
        EPS = 1e-05
        key = jax.random.key(seed)
        ks = jax.random.split(key, 12)
        x = jax.random.normal(ks[0], (B, N, D), dtype=jnp.float32)
        adj = jax.random.randint(ks[1], (B, N, N), 0, 2, dtype=jnp.int32)
        adj = jnp.maximum(adj, jnp.eye(N, dtype=jnp.int32)[None, :, :])
        s = 1.0 / np.sqrt(D)
        Wq = jax.random.uniform(ks[2], (D, D), jnp.float32, -s, s)
        bq = jnp.zeros((D,), jnp.float32)
        Wk = jax.random.uniform(ks[3], (D, D), jnp.float32, -s, s)
        bk = jnp.zeros((D,), jnp.float32)
        Wv = jax.random.uniform(ks[4], (D, D), jnp.float32, -s, s)
        bv = jnp.zeros((D,), jnp.float32)
        Wo = jax.random.uniform(ks[5], (D, D), jnp.float32, -s, s)
        bo = jnp.zeros((D,), jnp.float32)
        gamma = jnp.ones((D,), jnp.float32)
        beta = jnp.zeros((D,), jnp.float32)
        return {'x': x, 'adj': adj, 'Wq': Wq, 'bq': bq, 'Wk': Wk, 'bk': bk, 'Wv': Wv, 'bv': bv, 'Wo': Wo, 'bo': bo, 'gamma': gamma, 'beta': beta}
    _L1_gnn_all = _L1_gnn_setup()
    _L1_gnn_in = {k: v for k, v in _L1_gnn_all.items() if k in ('Wq', 'bq', 'Wk', 'bk', 'Wv', 'bv', 'Wo', 'bo', 'gamma', 'beta')}
    del _L1_gnn_all
    return {'x': x, 'adj': adj, 'L0_gnn_ln1_g': _L0_gnn_in['ln1_g'], 'L0_gnn_ln1_b': _L0_gnn_in['ln1_b'], 'L0_gnn_ln2_g': _L0_gnn_in['ln2_g'], 'L0_gnn_ln2_b': _L0_gnn_in['ln2_b'], 'L0_gnn_wq': _L0_gnn_in['wq'], 'L0_gnn_bq': _L0_gnn_in['bq'], 'L0_gnn_wk': _L0_gnn_in['wk'], 'L0_gnn_bk': _L0_gnn_in['bk'], 'L0_gnn_wv': _L0_gnn_in['wv'], 'L0_gnn_bv': _L0_gnn_in['bv'], 'L0_gnn_wo': _L0_gnn_in['wo'], 'L0_gnn_bo': _L0_gnn_in['bo'], 'L0_gnn_w1': _L0_gnn_in['w1'], 'L0_gnn_b1': _L0_gnn_in['b1'], 'L0_gnn_w2': _L0_gnn_in['w2'], 'L0_gnn_b2': _L0_gnn_in['b2'], 'L1_gnn_Wq': _L1_gnn_in['Wq'], 'L1_gnn_bq': _L1_gnn_in['bq'], 'L1_gnn_Wk': _L1_gnn_in['Wk'], 'L1_gnn_bk': _L1_gnn_in['bk'], 'L1_gnn_Wv': _L1_gnn_in['Wv'], 'L1_gnn_bv': _L1_gnn_in['bv'], 'L1_gnn_Wo': _L1_gnn_in['Wo'], 'L1_gnn_bo': _L1_gnn_in['bo'], 'L1_gnn_gamma': _L1_gnn_in['gamma'], 'L1_gnn_beta': _L1_gnn_in['beta']}

def reference(x, adj, L0_gnn_ln1_g, L0_gnn_ln1_b, L0_gnn_ln2_g, L0_gnn_ln2_b, L0_gnn_wq, L0_gnn_bq, L0_gnn_wk, L0_gnn_bk, L0_gnn_wv, L0_gnn_bv, L0_gnn_wo, L0_gnn_bo, L0_gnn_w1, L0_gnn_b1, L0_gnn_w2, L0_gnn_b2, L1_gnn_Wq, L1_gnn_bq, L1_gnn_Wk, L1_gnn_bk, L1_gnn_Wv, L1_gnn_bv, L1_gnn_Wo, L1_gnn_bo, L1_gnn_gamma, L1_gnn_beta):
    import jax
    import jax.numpy as jnp

    def _L0_gnn_ref(x, adj_matrix, edge_attr_matrix, ln1_g, ln1_b, ln2_g, ln2_b, wq, bq, wk, bk, wv, bv, wo, bo, w1, b1, w2, b2):
        import jax, jax.numpy as jnp
        import numpy as np
        B, S, D, H = (2, 1024, 256, 8)
        HD = D // H
        EPS = 1e-05

        def _ln(x, g, b):
            mu = jnp.mean(x, axis=-1, keepdims=True)
            var = jnp.mean((x - mu) ** 2, axis=-1, keepdims=True)
            return (x - mu) * jax.lax.rsqrt(var + EPS) * g + b
        b, s, d = x.shape
        residual = x
        nx = _ln(x, ln1_g, ln1_b)
        q = (nx @ wq + bq).reshape(b, s, H, HD).transpose(0, 2, 1, 3)
        k = (nx @ wk + bk).reshape(b, s, H, HD).transpose(0, 2, 1, 3)
        v = (nx @ wv + bv).reshape(b, s, H, HD).transpose(0, 2, 1, 3)
        adjf = adj_matrix.astype(jnp.float32)
        bias = jnp.where(adj_matrix > 0, 0.1 * edge_attr_matrix * adjf, -jnp.inf)[:, None]
        scores = jnp.einsum('bhqd,bhkd->bhqk', q, k) / np.sqrt(HD) + bias
        attn = jax.nn.softmax(scores, axis=-1)
        out = jnp.einsum('bhqk,bhkd->bhqd', attn, v)
        out = out.transpose(0, 2, 1, 3).reshape(b, s, d)
        x1 = residual + (out @ wo + bo)
        n2 = _ln(x1, ln2_g, ln2_b)
        mlp = jax.nn.gelu(n2 @ w1 + b1, approximate=False) @ w2 + b2
        return x1 + mlp

    def _L1_gnn_ref(x, adj, Wq, bq, Wk, bk, Wv, bv, Wo, bo, gamma, beta):
        import jax, jax.numpy as jnp
        import numpy as np
        B, N, D, H = (4, 1024, 256, 8)
        HD = D // H
        EPS = 1e-05
        b, n, d = x.shape
        scale = 1.0 / np.sqrt(HD).astype(np.float32)
        q = (x @ Wq + bq).reshape(b, n, H, HD)
        k = (x @ Wk + bk).reshape(b, n, H, HD)
        v = (x @ Wv + bv).reshape(b, n, H, HD)
        scores = jnp.einsum('bnhd,bmhd->bhnm', q, k) * scale
        mask = (adj == 0)[:, None, :, :]
        scores = jnp.where(mask, jnp.float32(-jnp.inf), scores)
        attn = jax.nn.softmax(scores, axis=-1)
        h = jnp.einsum('bhnm,bmhd->bnhd', attn, v).reshape(b, n, d)
        h = h @ Wo + bo
        y = h + x
        mu = jnp.mean(y, axis=-1, keepdims=True)
        var = jnp.mean(jnp.square(y - mu), axis=-1, keepdims=True)
        return (y - mu) * jax.lax.rsqrt(var + EPS) * gamma + beta
    x = _L0_gnn_ref(x, adj, adj, L0_gnn_ln1_g, L0_gnn_ln1_b, L0_gnn_ln2_g, L0_gnn_ln2_b, L0_gnn_wq, L0_gnn_bq, L0_gnn_wk, L0_gnn_bk, L0_gnn_wv, L0_gnn_bv, L0_gnn_wo, L0_gnn_bo, L0_gnn_w1, L0_gnn_b1, L0_gnn_w2, L0_gnn_b2)
    x = _L1_gnn_ref(x, adj, L1_gnn_Wq, L1_gnn_bq, L1_gnn_Wk, L1_gnn_bk, L1_gnn_Wv, L1_gnn_bv, L1_gnn_Wo, L1_gnn_bo, L1_gnn_gamma, L1_gnn_beta)
    return x

_drawn_inputs = setup_inputs


def setup_inputs(seed=0):
    import zlib

    import numpy as np

    out = dict(_drawn_inputs(seed))
    spreads = {'L0_gnn_ln1_g': (1.0, 0.2),
     'L0_gnn_ln1_b': (0.0, 0.1),
     'L0_gnn_ln2_g': (1.0, 0.2),
     'L0_gnn_ln2_b': (0.0, 0.1),
     'L0_gnn_bq': (0.0, 0.268),
     'L0_gnn_bk': (0.0, 0.8),
     'L0_gnn_bv': (0.0, 0.1),
     'L0_gnn_bo': (0.0, 0.1),
     'L0_gnn_b1': (0.0, 0.1),
     'L0_gnn_b2': (0.0, 0.1),
     'L1_gnn_bq': (0.0, 0.8),
     'L1_gnn_bk': (0.0, 0.8),
     'L1_gnn_bv': (0.0, 0.1),
     'L1_gnn_bo': (0.0, 0.1),
     'L1_gnn_gamma': (1.0, 0.2),
     'L1_gnn_beta': (0.0, 0.1)}
    factors = {}
    for name, (base, spread) in spreads.items():
        noise = np.random.default_rng([zlib.crc32(name.encode()), seed]).standard_normal(out[name].shape)
        drawn = base * np.exp(spread * noise) if base else spread * noise
        out[name] = jnp.asarray(drawn.astype(out[name].dtype))
    for name, factor in factors.items():
        out[name] = (out[name] * factor).astype(out[name].dtype)
    return out
```

```python
from contextlib import ExitStack

import numpy as np

import concourse.bass as bass
from concourse import mybir

F32 = mybir.dt.float32
F32R = mybir.dt.float32r
I32 = mybir.dt.int32
ALU = mybir.AluOpType
ACT = mybir.ActivationFunctionType

P = 128
B = 128
D = 256
H = 8
HD = D // H
KC = D // P
HC = H // KC
FF = 4 * D
FC = FF // P
GB = 4
TOK = GB * P
NG = B // GB
STEPS = 8
EPS = 1e-5
MASKED = 3.0e38
LARGEST = 3.4e38
BANKS = 4
HI, LO = 0, 1



def lags(steps, pending, drain):
    t, w, v = ([-1], [-2, -1], [-1]) if pending else ([], [], [])
    by_step = {}
    for r, k in enumerate(steps):
        ops = []
        if t:
            ops.append(("T", t.pop(0)))
        if w and w[0] <= r - 2:
            ops.append(("W", w.pop(0)))
        if v:
            ops.append(("V", v.pop(0)))
        t.append(r)
        w.append(r)
        v.append(r)
        by_step[k] = ops
    last = len(steps) - 1
    tail = [("T", last), ("W", last - 1), ("V", last), ("W", last)] if drain else []
    return by_step, tail


class Shape:

    def __init__(self, it, stages, following, before, drain):
        self.it, self.following, self.before, self.drain = it, following, before, drain
        self.a, self.m, self.c = ("A" in stages), ("M" in stages), ("C" in stages)
        self.units = {k: ("C", k) for k in range(GB)} if self.c else {}
        if self.a:
            self.units.update({GB + k: ("A", k) for k in range(GB)})
        self.steps = sorted(self.units)
        self.order = [self.units[k] for k in self.steps]
        self.looped = it == "loop"
        self.turns = NG - 3 if self.looped else 1
        pending = before is not None and not before.drain
        self.lag, self.tail = lags(self.steps, pending, drain)
        a, m = self.a, self.m
        self.mid = {0: [("XT", "A")] * a, 3: [("Q", "A")] * a + [("XT", "M")] * m,
                    5: [("XT", "C")] * m, 7: [("Q", "C")] * m}
        self.fill = {0: [("K", "A")] * a, 1: [("V", "A")] * a,
                     3: [("UP", None), ("DOWN", 0)] * m, 4: [("DOWN", 1)] * m,
                     5: [("K", "C")] * m, 7: [("V", "C")] * m}
        self.use, self.high = {}, {}
        for k in range(STEPS):
            self.number(self.mid.get(k, []), self.lag.get(k, []), self.fill.get(k, []))
            if k == self.steps[-1]:
                self.number([], self.tail, [])
        if before is None:
            self.unit0 = self.use0 = self.high0 = 0
        else:
            self.unit0 = before.unit0 + before.turns * len(before.order)
            self.use0 = before.use0 + before.turns * len(before.use)
            self.high0 = before.high0 + before.turns * len(before.high)
        assert not self.looped or len(self.use) % BANKS == 0

    def number(self, mid, lagging, fill):
        middle = [x for op in mid for x in bank_uses(op)]
        late = [("W" if o == "W" else "O", r) for o, r in lagging if o != "T"]
        final = [x for op in fill for x in bank_uses(op)]
        for x in middle + late + final:
            self.use[x] = len(self.use)
            if x[0] in ("XT", "Q", "K", "O"):
                self.high[x] = len(self.high)


def bank_uses(op):
    kind, what = op
    if kind == "UP":
        return [("UP", j) for j in range(FC)]
    if kind == "DOWN":
        return [("DOWN", what)]
    return [(kind, what, i) for i in range(2)]


def make_shapes():
    shapes, before = [], None
    for it, stages, following in [(0, "A", True), (1, "AM", True), ("loop", "AMC", True),
                                  (NG - 1, "AMC", False), (NG, "MC", False), (NG + 1, "C", False)]:
        before = Shape(it, stages, following, before, it in (0, NG, NG + 1))
        shapes.append(before)
    return shapes


class Turn:

    def __init__(self, shape, it):
        self.s, self.it = shape, it
        self.group_a, self.group_m, self.group_c = it, it - 1, it - 2

    def grown(self, base, each):
        return self.it * each + (base - 2 * each) if self.s.looped else base

    def unit(self, r):
        order = self.s.order if r >= 0 else self.s.before.order
        stage, b = order[r]
        return self.grown(self.s.unit0 + r, len(self.s.order)), stage, b

    def group(self, r):
        _, stage, _ = self.unit(r)
        return (self.group_a if stage == "A" else self.group_c) - (1 if r < 0 else 0)

    def bank(self, key, earlier=False):
        s = self.s
        n = s.use0 + (s.before.use[key] - len(s.before.use) if earlier else s.use[key])
        return n % BANKS, self.grown(n // BANKS + 1, len(s.use) // BANKS)

    def bank_of_values(self, r):
        if ("O", r) in self.s.use:
            return self.bank(("O", r))
        return self.bank(("O", len(self.s.before.order) + r), earlier=True)

    def high(self, key):
        return self.grown(self.s.high0 + self.s.high[key] + 1, len(self.s.high))


def run_pipeline(eng, shapes, body):
    for s in shapes:
        if s.looped:
            with eng.Fori(2, NG - 1) as it:
                body(Turn(s, it))
        else:
            body(Turn(s, s.it))


def wait(eng, sem, count):
    if not (isinstance(count, int) and count <= 0):
        eng.wait_ge(sem, count)


def build(nc, T, out):
    ctx = ExitStack()
    with ctx:
        def sb(name, shape, dt=F32):
            return ctx.enter_context(nc.sbuf_tensor(name, shape, dt))

        def sem(name):
            return ctx.enter_context(nc.semaphore(name))

        weight = {}
        for name in ("q0", "k0", "v0", "o0", "q1", "k1", "v1", "o1"):
            weight[name] = sb("w_" + name, [P, 2, KC, D], F32R)
        w_up = sb("w_up", [P, 2, KC, FF], F32R)
        w_down = sb("w_down", [P, 2, FC, D], F32R)
        bias_row = {n: sb("bias_" + n, [P, D], F32R) for n in ("o0", "down", "o1")}
        pick = sb("pick", [P, P], F32R)
        ident = sb("ident", [P, P])
        gamma, beta = sb("gamma", [P, D]), sb("beta", [P, D])
        cols = sb("cols", [P, 28])
        ready_cols = sb("ready_cols", [P, 16])
        half, fence = sb("half", [P, GB]), sb("fence", [P, 16])

        normed = sb("normed", [P, 2, KC, TOK], F32R)
        queries = sb("queries", [P, 2, KC, TOK], F32R)
        keys = sb("keys", [P, 2, KC, TOK], F32R)
        key_blocks = sb("key_blocks", [P, 2, KC, HC, TOK], F32R)
        values = {"A": sb("values_a", [P, GB, D]), "C": sb("values_c", [P, GB, D])}
        scores = sb("scores", [P, 2, H, P])
        negmax, total, inverse = sb("negmax", [P, 2, H]), sb("total", [P, 2, H]), sb("inverse", [P, 2, H])
        probs_t = sb("probs_t", [P, H, P])
        heads_t = sb("heads_t", [P, 2, KC, P], F32R)
        hidden_raw = sb("hidden_raw", [P, 2, TOK])
        hidden = sb("hidden", [P, 2, FC, TOK], F32R)
        x_in = sb("x_in", [P, GB, D])
        res_a = sb("res_a", [P, GB, D])
        x_two = sb("x_two", [P, GB, D])
        res_c = sb("res_c", [P, GB, D])
        adj = {"A": sb("adj_a", [P, GB, P]), "C": sb("adj_c", [P, GB, P])}
        adj_tmp = sb("adj_tmp", [P, GB, P])
        stats = {n: sb("stats_" + n, [P, GB, 6]) for n in "AMC"}
        moments = {n: sb("moments_" + n, [P, GB, 2]) for n in "AMC"}
        spread = {n: sb("spread_" + n, [P, GB]) for n in "AMC"}
        rstd = {n: sb("rstd_" + n, [P, GB]) for n in "AMC"}

        p_scores = ctx.enter_context(nc.psum_tensor("p_scores", [P, KC, HC * P], F32))
        p_probs = ctx.enter_context(nc.psum_tensor("p_probs", [P, KC, HC * P], F32))
        p_bank = [ctx.enter_context(nc.psum_tensor(f"p_bank{i}", [P, TOK], F32)) for i in range(BANKS)]

        piece_loaded, cols_loaded = [sem("piece_loaded0"), sem("piece_loaded1")], sem("cols_loaded")
        consts_ready, piece_scaled, piece_high = sem("consts_ready"), sem("piece_scaled"), sem("piece_high")
        piece_done, bias_products, setup_vector = sem("piece_done"), sem("bias_products"), sem("setup_vector")
        zeroed, bias_summed = sem("zeroed"), sem("bias_summed")
        x_loaded, res_a_loaded, res_c_loaded = sem("x_loaded"), sem("res_a_loaded"), sem("res_c_loaded")
        adj_loaded = {"A": sem("adj_a_loaded"), "C": sem("adj_c_loaded")}
        blocks_loaded = {"A": sem("blocks_a_loaded"), "C": sem("blocks_c_loaded")}
        stored = sem("stored")
        filled = [sem(f"filled{i}") for i in range(BANKS)]
        scores_made, probs_turned = sem("scores_made"), sem("probs_turned")
        drained = [sem(f"drained{i}") for i in range(BANKS)]
        high_made, exps_made, turned_out0 = sem("high_made"), sem("exps_made"), sem("turned_out0")
        masked_made, inverses_made, turned_out1 = sem("masked_made"), sem("inverses_made"), sem("turned_out1")
        hidden_high, hidden_made = sem("hidden_high"), sem("hidden_made")
        ln_steps = {n: sem("ln_steps_" + n) for n in "AMC"}
        ln_applied = {n: sem("ln_applied_" + n) for n in "AMC"}
        mask_steps = {"A": sem("mask_steps_a"), "C": sem("mask_steps_c")}
        probs_made, gained, finished = sem("probs_made"), sem("gained"), sem("finished")
        rstd_made = {n: sem("rstd_made_" + n) for n in "AMC"}

        x_view = T["x"].rearrange("b s d -> s b d")
        out_view = out.rearrange("b s d -> s b d")
        adj_view = T["adj"].rearrange("b q k -> q b k")

        def w_view(name):
            return T[name].rearrange("(c p) n -> p c n", p=P)

        L0, L1 = "L0_gnn_", "L1_gnn_"
        vectors = [(L0 + "ln1_g", KC), (L0 + "ln2_g", KC), (L0 + "ln1_b", KC), (L0 + "ln2_b", KC),
                   (L0 + "bq", KC), (L0 + "bk", KC), (L0 + "bv", KC), (L0 + "b1", FC),
                   (L1 + "bq", KC), (L1 + "bk", KC), (L1 + "bv", KC)]
        at, col = {}, 0
        for name, n in vectors:
            at[name] = col
            col += n
        assert col == cols.shape[1]
        rows = [("o0", L0 + "bo"), ("down", L0 + "b2"), ("o1", L1 + "bo")]
        QSCALE = -1.0 / float(np.sqrt(HD))

        W = KC * D
        flat = lambda t: t.rearrange("p c n -> p (c n)")
        whole = lambda name: (lambda part: flat(weight[name][:, part]))
        staged = [scores[:, i].rearrange("p h n -> p (h n)") for i in range(2)]
        scaled = probs_t[:, :, :].rearrange("p h n -> p (h n)")
        w1, w2 = w_view(L0 + "w1"), w_view(L0 + "w2")
        g1 = [cols[:, at[L0 + "ln1_g"] + c:at[L0 + "ln1_g"] + c + 1] for c in range(KC)]
        g2 = [cols[:, at[L0 + "ln2_g"] + c:at[L0 + "ln2_g"] + c + 1] for c in range(KC)]
        pieces = [
            ([w_view(L0 + "wq"), w_view(L0 + "wk")], [whole("q0"), whole("k0")],
             [(0, D, g1[0], QSCALE), (D, D, g1[1], QSCALE), (2 * D, D, g1[0], 1.0), (3 * D, D, g1[1], 1.0)]),
            ([w_view(L0 + "wv"), w_view(L0 + "wo")], [whole("v0"), whole("o0")],
             [(0, D, g1[0], 1.0), (D, D, g1[1], 1.0), (2 * D, 2 * D, 1.0, 1.0)]),
            ([w1[:, 0:1]], [lambda part: w_up[:, part, 0]], [(0, FF, g2[0], 1.0)]),
            ([w1[:, 1:2]], [lambda part: w_up[:, part, 1]], [(0, FF, g2[1], 1.0)]),
            ([w2[:, 0:4]], [lambda part: flat(w_down[:, part, 0:4])], [(0, FF, 1.0, 1.0)]),
            ([w2[:, 4:8]], [lambda part: flat(w_down[:, part, 4:8])], [(0, FF, 1.0, 1.0)]),
            ([w_view(L1 + "Wq"), w_view(L1 + "Wk")], [whole("q1"), whole("k1")],
             [(0, W, 1.0, QSCALE), (W, W, 1.0, 1.0)]),
            ([w_view(L1 + "Wv"), w_view(L1 + "Wo")], [whole("v1"), whole("o1")], [(0, 2 * W, 1.0, 1.0)]),
        ]
        loaded_by = [16 * sum(len(pieces[m][0]) for m in range(n % 2, n + 1, 2)) for n in range(len(pieces))]
        ZEROED = 8
        SETUP_VECTOR = 23
        spread_bv = adj_tmp
        row_raw = res_c

        def setup_over(eng):
            eng.wait_ge(piece_done, len(pieces))
            eng.wait_ge(setup_vector, SETUP_VECTOR)
            eng.wait_ge(zeroed, ZEROED)

        shapes = make_shapes()
        weights_of = {"A": ("q0", "k0", "v0", "o0"), "C": ("q1", "k1", "v1", "o1")}
        residual = {"A": res_a, "C": res_c}
        bias_of = {"A": "o0", "C": "o1"}
        block = ctx.enter_context(nc.Block())

        @block.sync
        def _(sp):
            for name, n in vectors:
                sp.dma_start(cols[:, at[name]:at[name] + n], T[name].rearrange("(c p) -> p c", p=P),
                             allow_slow_non_contiguous=True).then_inc(cols_loaded, 16)
            for i, (_, name) in enumerate(rows):
                sp.dma_start(row_raw[:, i, :], T[name].partition_broadcast(P)).then_inc(cols_loaded, 16)
            sp.dma_start(gamma[:, :], T[L1 + "gamma"].partition_broadcast(P)).then_inc(cols_loaded, 16)
            sp.dma_start(beta[:, :], T[L1 + "beta"].partition_broadcast(P)).then_inc(cols_loaded, 16)
            for n, (loads, _, _) in enumerate(pieces):
                if n >= 2:
                    sp.wait_ge(piece_scaled, n - 1)
                    sp.wait_ge(bias_products, n)
                for i, src in enumerate(loads):
                    width = 2 * W // len(loads)
                    dst = staged[n % 2][:, i * width:(i + 1) * width].rearrange("p (c n) -> p c n", n=src.shape[2])
                    sp.dma_start(dst, src).then_inc(piece_loaded[n % 2], 16)
                if n == 1:
                    sp.dma_start(x_in[:, :, :], x_view[:, 0:GB, :]).then_inc(x_loaded, 16)
                    sp.dma_start(adj["A"][:, :, :].bitcast(I32), adj_view[:, 0:GB, :]).then_inc(adj_loaded["A"], 16)
            setup_over(sp)

            def drained_use(t, use):
                bank, number = t.bank(use)
                return drained[bank], number

            def load_blocks(stage, condition):
                sp.wait_ge(*condition)
                for j in range(HC):
                    rows_j = slice(HD * j, HD * (j + 1))
                    sp.dma_start(key_blocks[rows_j, :, :, j, :].bitcast(F32), keys[rows_j, :, :, :].bitcast(F32)
                                 ).then_inc(blocks_loaded[stage], 16)

            def store(t, b):
                sp.wait_ge(finished, t.group_c * GB + b + 1)
                sp.dma_start(out_view[:, bass.ds(t.group_c * GB + b, 1), :], res_c[:, b:b + 1, :]).then_inc(stored, 16)

            def body(t):
                s = t.s
                unit0 = t.grown(s.unit0, len(s.order))
                if s.a and s.following:
                    sp.wait_ge(*drained_use(t, ("XT", "A", 1)))
                    sp.dma_start(x_in[:, :, :], x_view[:, bass.ds((t.group_a + 1) * GB, GB), :]).then_inc(x_loaded, 16)
                if s.a:
                    load_blocks("A", (masked_made, (unit0 + GB) * H) if s.c else drained_use(t, ("K", "A", 1)))
                if s.c:
                    store(t, 0)
                    store(t, 1)
                if s.m:
                    if s.c:
                        sp.wait_ge(masked_made, (unit0 + GB) * H)
                    sp.dma_start(adj["C"][:, :, :].bitcast(I32), adj_view[:, bass.ds(t.group_m * GB, GB), :]
                                 ).then_inc(adj_loaded["C"], 16)
                if s.a:
                    if s.m:
                        sp.wait_ge(*drained_use(t, ("DOWN", 1)))
                    sp.dma_start(res_a[:, :, :], x_view[:, bass.ds(t.group_a * GB, GB), :]).then_inc(res_a_loaded, 16)
                if s.c:
                    store(t, 2)
                    store(t, 3)
                if s.m:
                    if s.c:
                        sp.wait_ge(stored, (t.group_c + 1) * GB * 16)
                    if not (s.a and s.c):
                        sp.wait_ge(*drained_use(t, ("DOWN", 1)))
                    sp.dma_start(res_c[:, :, :], x_two[:, :, :]).then_inc(res_c_loaded, 16)
                    load_blocks("C", (masked_made, (unit0 + len(s.order)) * H) if s.a
                                else drained_use(t, ("K", "C", 1)))
                if s.a and s.following:
                    sp.wait_ge(masked_made, (unit0 + len(s.order)) * H)
                    sp.dma_start(adj["A"][:, :, :].bitcast(I32), adj_view[:, bass.ds((t.group_a + 1) * GB, GB), :]
                                 ).then_inc(adj_loaded["A"], 16)

            run_pipeline(sp, shapes, body)
            sp.wait_ge(stored, NG * GB * 16)

        @block.gpsimd
        def _(pool):
            nc.gpsimd.memset(ident[:, :], 0.0).then_inc(zeroed, 1)
            nc.gpsimd.memset(half[:, :], -0.5).then_inc(zeroed, 1)
            for t in bias_row.values():
                last = nc.gpsimd.memset(t[:, :].bitcast(F32), 0.0)
            last.then_inc(zeroed, 1)
            nc.gpsimd.memset(pick[:, :].bitcast(F32), 0.0).then_inc(zeroed, 1)
            pool.wait_ge(zeroed, 4)
            nc.gpsimd.affine_select(out=ident[:, :], in_=ident[:, :], compare_op=ALU.not_equal, fill=1.0,
                                    base=0, pattern=[[-1, P]], channel_multiplier=1).then_inc(zeroed, 1)
            pool.wait_ge(zeroed, 5)
            nc.gpsimd.memset(pick[0:1, :].bitcast(F32), 1.0).then_inc(zeroed, 1)
            pool.wait_ge(zeroed, 6)
            nc.gpsimd.memset(pick[32:33, :].bitcast(F32), 1.0).then_inc(zeroed, 1)
            pool.wait_ge(zeroed, 7)
            nc.gpsimd.memset(key_blocks[:, :, :, :, :].bitcast(F32), 0.0).then_inc(zeroed, 1)

            def make_rstd(n, b0, b1, steps):
                pool.wait_ge(ln_steps[n], steps)
                nc.gpsimd.tensor_tensor(rstd[n][:, b0:b1], spread[n][:, b0:b1], half[:, b0:b1], ALU.pow
                                        ).then_inc(rstd_made[n], 1)

            make_rstd("A", 0, GB, 3)
            setup_over(pool)

            def after(t, ops):
                for op, r in ops:
                    if op != "W":
                        continue
                    _, stage, b = t.unit(r)
                    if stage == "A" and b == GB - 1:
                        make_rstd("M", 0, GB, t.group(r) * 3 + 3)
                    if stage == "C":
                        unit = t.group(r) * GB + b
                        make_rstd("C", b, b + 1, unit * 3 + 3)
                        pool.wait_ge(ln_applied["C"], unit + 1)
                        nc.gpsimd.tensor_tensor(res_c[:, b], res_c[:, b], gamma[:, :], ALU.mult).then_inc(gained, 1)
                        pool.wait_ge(gained, unit + 1)
                        nc.gpsimd.tensor_tensor(res_c[:, b], res_c[:, b], beta[:, :], ALU.add).then_inc(finished, 1)

            def body(t):
                s = t.s
                for k in range(STEPS):
                    if k in s.units:
                        u, _, _ = t.unit(s.steps.index(k))
                        for c in range(KC):
                            pool.wait_ge(inverses_made, u * KC + c + 1)
                            heads = slice(HC * c, HC * (c + 1))
                            rows_c = scores[:, k % 2, heads, :]
                            nc.gpsimd.tensor_tensor(
                                rows_c, rows_c, inverse[:, k % 2, heads].unsqueeze(2).broadcast_to([P, HC, P]),
                                ALU.mult).then_inc(probs_made, 1)
                    after(t, s.lag.get(k, []))
                    if k == 6 and s.following:
                        make_rstd("A", 0, GB, (t.group_a + 1) * 3 + 3)
                    if k == s.steps[-1]:
                        after(t, s.tail)

            run_pipeline(pool, shapes, body)

        @block.scalar
        def _(act):
            for n, (_, targets, _) in enumerate(pieces):
                act.wait_ge(piece_scaled, n + 1)
                width = 2 * W // len(targets)
                for i, target in enumerate(targets):
                    last = nc.scalar.activation(target(HI), scaled[:, i * width:(i + 1) * width], ACT.Copy)
                last.then_inc(piece_high, 1)
            setup_over(act)

            def exps(t, k, c):
                u, _, _ = t.unit(t.s.steps.index(k))
                for h in range(HC * c, HC * (c + 1)):
                    if h % 2 == 0:
                        act.wait_ge(masked_made, u * H + h + 2)
                    last = nc.scalar.activation(scores[:, k % 2, h], scores[:, k % 2, h], ACT.Exp, scale=-1.0,
                                                bias=negmax[:, k % 2, h:h + 1], accum_out=total[:, k % 2, h:h + 1])
                last.then_inc(exps_made, 1)

            def evacuate(t, op):
                kind, what = op
                for use in bank_uses(op):
                    bank, number = t.bank(use)
                    src = p_bank[bank]
                    act.wait_ge(filled[bank], number)
                    if kind == "XT":
                        nc.scalar.activation(normed[:, HI, use[2], :], src[:, :], ACT.Copy).then_inc(high_made, 1)
                    elif kind in "QK":
                        if kind == "K":
                            if what == "A" and t.s.c:
                                act.wait_ge(blocks_loaded["C"], (t.group_c + 1) * HC * 16)
                            elif what == "A":
                                wait(act, blocks_loaded["A"], t.group_a * HC * 16)
                            elif t.s.a:
                                act.wait_ge(blocks_loaded["A"], (t.group_a + 1) * HC * 16)
                            else:
                                act.wait_ge(blocks_loaded["C"], (t.group_c + 1) * HC * 16)
                        bias = 4 * (what == "C") + 2 * (kind == "K") + use[2]
                        dst = queries if kind == "Q" else keys
                        nc.scalar.activation(dst[:, HI, use[2], :], src[:, :], ACT.Identity,
                                             bias=ready_cols[:, bias:bias + 1]).then_inc(high_made, 1)
                    elif kind == "V":
                        dst = values[what][:, 2 * use[2]:2 * use[2] + 2, :].rearrange("p g n -> p (g n)")
                        nc.scalar.activation(dst, src[:, :], ACT.Copy).then_inc(drained[bank], 1)
                    elif kind == "UP":
                        j = use[1]
                        wait(act, hidden_made, t.group_m * FC + j - 1)
                        nc.scalar.activation(hidden_raw[:, j % 2], src[:, :], ACT.Gelu,
                                             bias=ready_cols[:, 8 + j:9 + j]).then_inc(drained[bank], 1)

            def turned(t, r):
                u, _, _ = t.unit(r)
                act.wait_ge(probs_turned, u * KC + 1)
                nc.scalar.activation(probs_t[:, 0:HC].rearrange("p h n -> p (h n)"), p_probs[:, 0, :], ACT.Copy
                                     ).then_inc(turned_out0, 1)

            def heads_high(t, r):
                bank, number = t.bank(("O", r))
                act.wait_ge(filled[bank], number)
                nc.scalar.activation(heads_t[:, HI].rearrange("p c n -> p (c n)"), p_bank[bank][:, 0:KC * P],
                                     ACT.Copy).then_inc(high_made, 1)

            def body(t):
                s = t.s
                for k in range(STEPS):
                    lag = s.lag.get(k, [])
                    if k in s.units:
                        exps(t, k, 0)
                    for op in s.mid.get(k, []):
                        evacuate(t, op)
                    for op, r in lag:
                        if op == "T":
                            turned(t, r)
                    if k in s.units:
                        exps(t, k, 1)
                    for op, r in lag:
                        if op == "V":
                            heads_high(t, r)
                    for op in s.fill.get(k, []):
                        if op[0] != "DOWN":
                            evacuate(t, op)
                    for op, r in s.tail if k == s.steps[-1] else []:
                        if op == "T":
                            turned(t, r)
                        if op == "V":
                            heads_high(t, r)

            run_pipeline(act, shapes, body)

        @block.vector
        def _(dve):
            step, taken = [0], [0]

            def then(instruction):
                step[0] += 1
                instruction.then_inc(setup_vector, 1)
                dve.wait_ge(setup_vector, step[0])

            def take_wait():
                at_col = taken[0] % fence.shape[1]
                taken[0] += 1
                nc.vector.memset(fence[:, at_col:at_col + 1], 0.0)

            def layer_norm_steps(n, src, b0, b1, done, measure):
                if measure:
                    for b in range(b0, b1):
                        last = nc.vector.bn_stats(stats[n][:, b, :], src[:, b, :])
                    last.then_inc(ln_steps[n], 1)
                dve.wait_ge(ln_steps[n], done + 1)
                take_wait()
                for b in range(b0, b1):
                    last = nc.vector.bn_aggr(moments[n][:, b, :], stats[n][:, b, :])
                last.then_inc(ln_steps[n], 1)
                dve.wait_ge(ln_steps[n], done + 2)
                nc.vector.tensor_scalar(spread[n][:, b0:b1], moments[n][:, b0:b1, 1], EPS, None, ALU.add
                                        ).then_inc(ln_steps[n], 1)

            def normalize(n, src, dst, b0, b1, made):
                dve.wait_ge(rstd_made[n], made)
                for b in range(b0, b1):
                    last = nc.vector.tensor_scalar(dst[:, b, :], src[:, b, :], moments[n][:, b, 0:1],
                                                   rstd[n][:, b:b + 1], ALU.subtract, ALU.mult)
                last.then_inc(ln_applied[n], 1)

            def mask_a(group):
                a = adj["A"][:, :, :]
                dve.wait_ge(adj_loaded["A"], (group + 1) * 16)
                nc.vector.scalar_tensor_tensor(out=adj_tmp[:, :, :], in0=a.bitcast(I32), scalar=-0.1,
                                               in1=a.bitcast(I32), op0=ALU.mult, op1=ALU.mult
                                               ).then_inc(mask_steps["A"], 1)
                dve.wait_ge(mask_steps["A"], group * 3 + 1)
                nc.vector.tensor_scalar(a, a.bitcast(I32), 0.0, MASKED, ALU.is_le, ALU.mult
                                        ).then_inc(mask_steps["A"], 1)
                dve.wait_ge(mask_steps["A"], group * 3 + 2)
                nc.vector.tensor_tensor(a, a, adj_tmp[:, :, :], ALU.add).then_inc(mask_steps["A"], 1)
                dve.wait_ge(mask_steps["A"], group * 3 + 3)

            def mask_c(group):
                a = adj["C"][:, :, :]
                dve.wait_ge(adj_loaded["C"], (group + 1) * 16)
                nc.vector.tensor_scalar(a, a.bitcast(I32), 0.0, MASKED, ALU.is_equal, ALU.mult
                                        ).then_inc(mask_steps["C"], 1)
                dve.wait_ge(mask_steps["C"], group + 1)

            dve.wait_ge(cols_loaded, 16 * (len(vectors) + len(rows) + 2))
            dve.wait_ge(zeroed, ZEROED - 1)

            def bias_rows(i, name, psum):
                t = row_raw[:, i, :]
                if psum is not None:
                    then(nc.vector.tensor_tensor(t, psum, t, ALU.add))
                nc.vector.tensor_copy(bias_row[name][0:1, :], t[0:1, :])
                then(nc.vector.tensor_copy(bias_row[name][32:33, :], t[32:33, :]))
                then(nc.vector.tensor_tensor(bias_row[name][32:33, :], t[32:33, :],
                                             bias_row[name][32:33, :].bitcast(F32), ALU.subtract))

            then(nc.vector.memset(spread_bv[:, :, :], 1.0))
            for c in range(KC):
                q, bk, bv = at[L1 + "bq"] + c, at[L1 + "bk"] + c, at[L1 + "bv"] + c
                then(nc.vector.tensor_scalar(ready_cols[:, 4 + c:5 + c], cols[:, q:q + 1], QSCALE, None, ALU.mult))
                then(nc.vector.tensor_copy(ready_cols[:, 6 + c:7 + c], cols[:, bk:bk + 1]))
                then(nc.vector.tensor_scalar(spread_bv[:, KC + c, :], spread_bv[:, KC + c, :], cols[:, bv:bv + 1],
                                             None, ALU.mult))
            bias_rows(1, "down", None)
            biases = cols[:, at[L0 + "bq"]:at[L0 + "bq"] + 3 * KC]
            up_bias = cols[:, at[L0 + "b1"]:at[L0 + "b1"] + FC]
            for n, (_, targets, factors) in enumerate(pieces):
                dve.wait_ge(piece_loaded[n % 2], loaded_by[n])
                if n:
                    dve.wait_ge(piece_high, n)
                    dve.wait_ge(piece_done, n)
                for start, width, gain, factor in factors:
                    last = nc.vector.tensor_scalar(scaled[:, start:start + width], staged[n % 2][:, start:start + width],
                                                   gain, factor, ALU.mult, ALU.mult)
                last.then_inc(piece_scaled, 1)
                dve.wait_ge(piece_high, n + 1)
                width = 2 * W // len(targets)
                for i, target in enumerate(targets):
                    last = nc.vector.tensor_tensor(target(LO), scaled[:, i * width:(i + 1) * width],
                                                   target(HI).bitcast(F32), ALU.subtract)
                last.then_inc(piece_done, 1)
                if n == 1:
                    dve.wait_ge(bias_products, 2)
                    sums = p_bank[0][:, 0:3 * KC * KC].rearrange("p (x c) -> p c x", c=KC)
                    then(nc.vector.tensor_tensor(biases, sums[:, 0], biases, ALU.add))
                    then(nc.vector.tensor_tensor(biases, sums[:, 1], biases, ALU.add))
                    then(nc.vector.tensor_scalar(ready_cols[:, 0:2], biases[:, 0:2], QSCALE, None, ALU.mult))
                    then(nc.vector.tensor_copy(ready_cols[:, 2:4], biases[:, 2:4]))
                    for c in range(KC):
                        then(nc.vector.tensor_scalar(spread_bv[:, c, :], spread_bv[:, c, :], biases[:, 4 + c:5 + c],
                                                     None, ALU.mult))
                    nc.vector.memset(spread["C"][:, :], 1.0).then_inc(bias_summed, 1)
                if n == 2:
                    dve.wait_ge(bias_products, 3)
                    bias_rows(0, "o0", p_bank[1][:, 0:D])
                if n == 3:
                    dve.wait_ge(bias_products, 4)
                    sums = p_bank[3][:, 0:FC * KC].rearrange("p (c x) -> p c x", c=KC)
                    then(nc.vector.tensor_tensor(up_bias, sums[:, 0], up_bias, ALU.add))
                    then(nc.vector.tensor_tensor(ready_cols[:, 8:16], sums[:, 1], up_bias, ALU.add))
            dve.wait_ge(bias_products, len(pieces))
            bias_rows(2, "o1", p_bank[2][:, 0:D])
            assert step[0] == SETUP_VECTOR, step[0]
            dve.wait_ge(x_loaded, 16)
            layer_norm_steps("A", x_in, 0, GB, 0, True)
            normalize("A", x_in, x_in, 0, GB, 1)
            mask_a(0)
            setup_over(dve)

            def mask_scores(t, k):
                u, stage, b = t.unit(t.s.steps.index(k))
                for h in range(H):
                    if h % HC == 0:
                        dve.wait_ge(scores_made, u * KC + h // HC + 1)
                        take_wait()
                    nc.vector.tensor_tensor_reduce(
                        out=scores[:, k % 2, h], in0=p_scores[:, h // HC, (h % HC) * P:(h % HC + 1) * P],
                        in1=adj[stage][:, b, :], scale=1.0, scalar=LARGEST, op0=ALU.add, op1=ALU.min,
                        accum_out=negmax[:, k % 2, h:h + 1]).then_inc(masked_made, 1)

            def evacuate(t, op):
                kind, what = op
                for use in bank_uses(op):
                    bank, number = t.bank(use)
                    src = p_bank[bank]
                    if kind == "XT":
                        dve.wait_ge(high_made, t.high(use))
                        hi, lo = normed[:, HI, use[2], :], normed[:, LO, use[2], :]
                        nc.vector.tensor_tensor(lo, src[:, :], hi.bitcast(F32), ALU.subtract).then_inc(drained[bank], 1)
                    elif kind in "QK":
                        dve.wait_ge(high_made, t.high(use))
                        bias = 4 * (what == "C") + 2 * (kind == "K") + use[2]
                        dst = queries if kind == "Q" else keys
                        nc.vector.scalar_tensor_tensor(
                            out=dst[:, LO, use[2], :], in0=src[:, :], scalar=ready_cols[:, bias:bias + 1],
                            in1=dst[:, HI, use[2], :].bitcast(F32), op0=ALU.add, op1=ALU.subtract
                        ).then_inc(drained[bank], 1)
                    elif kind == "UP":
                        j = use[1]
                        dve.wait_ge(drained[bank], number)
                        nc.vector.tensor_copy(hidden[:, HI, j, :], hidden_raw[:, j % 2]).then_inc(hidden_high, 1)
                        dve.wait_ge(hidden_high, t.group_m * FC + j + 1)
                        nc.vector.tensor_tensor(hidden[:, LO, j, :], hidden_raw[:, j % 2],
                                                hidden[:, HI, j, :].bitcast(F32), ALU.subtract
                                                ).then_inc(hidden_made, 1)
                    elif kind == "DOWN":
                        dve.wait_ge(filled[bank], number)
                        two = slice(2 * what, 2 * what + 2)
                        both = lambda x: x[:, two, :].rearrange("p g n -> p (g n)")
                        nc.vector.tensor_tensor(both(x_two), src[:, :], both(res_a), ALU.add
                                                ).then_inc(drained[bank], 1)

            def turned(t, r):
                u, _, _ = t.unit(r)
                dve.wait_ge(probs_turned, u * KC + 2)
                nc.vector.tensor_copy(probs_t[:, HC:H].rearrange("p h n -> p (h n)"), p_probs[:, 1, :]
                                      ).then_inc(turned_out1, 1)

            def heads_low(t, r):
                bank, _ = t.bank(("O", r))
                dve.wait_ge(high_made, t.high(("O", r)))
                part = lambda i: heads_t[:, i].rearrange("p c n -> p (c n)")
                nc.vector.tensor_tensor(part(LO), p_bank[bank][:, 0:KC * P], part(HI).bitcast(F32), ALU.subtract
                                        ).then_inc(drained[bank], 1)

            def add_residual(t, r):
                _, stage, b = t.unit(r)
                group = t.group(r)
                bank, number = t.bank(("W", r))
                dve.wait_ge(filled[bank], number)
                dve.wait_ge(res_a_loaded if stage == "A" else res_c_loaded, (group + 1) * 16)
                x = residual[stage]
                nc.vector.tensor_tensor(x[:, b, :], p_bank[bank][:, 0:D], x[:, b, :], ALU.add
                                        ).then_inc(drained[bank], 1)
                dve.wait_ge(drained[bank], number)
                if stage == "C":
                    layer_norm_steps("C", x, b, b + 1, (group * GB + b) * 3, True)
                else:
                    last = nc.vector.bn_stats(stats["M"][:, b, :], x[:, b, :])
                    if b == GB - 1:
                        last.then_inc(ln_steps["M"], 1)
                        layer_norm_steps("M", x, 0, GB, group * 3, False)

            def apply_norm(t, r):
                _, stage, b = t.unit(r)
                group = t.group(r)
                if stage == "C":
                    normalize("C", res_c, res_c, b, b + 1, group * GB + b + 1)
                elif b == GB - 1:
                    wait(dve, res_c_loaded, group * 16)
                    normalize("M", res_a, x_two, 0, GB, group + 1)

            def body(t):
                s = t.s
                for k in range(STEPS):
                    lag = s.lag.get(k, [])
                    if k in s.units:
                        mask_scores(t, k)
                    for op in s.mid.get(k, []):
                        evacuate(t, op)
                    for op, r in lag:
                        if op == "T":
                            turned(t, r)
                    if k in s.units:
                        u, _, _ = t.unit(s.steps.index(k))
                        dve.wait_ge(exps_made, u * KC + 1)
                        nc.vector.reciprocal(inverse[:, k % 2, 0:HC], total[:, k % 2, 0:HC]).then_inc(inverses_made, 1)
                    for op, r in lag:
                        if op == "W":
                            add_residual(t, r)
                    if k in s.units:
                        dve.wait_ge(exps_made, u * KC + 2)
                        nc.vector.reciprocal(inverse[:, k % 2, HC:H], total[:, k % 2, HC:H]).then_inc(inverses_made, 1)
                    for op, r in lag:
                        if op == "V":
                            heads_low(t, r)
                    for op in s.fill.get(k, []):
                        evacuate(t, op)
                    for op, r in lag:
                        if op == "W":
                            apply_norm(t, r)
                    if k == 1 and s.a and s.before is not None:
                        mask_a(t.group_a)
                    if k == 5 and s.m:
                        mask_c(t.group_m)
                    if k == 6 and s.following:
                        dve.wait_ge(x_loaded, (t.group_a + 2) * 16)
                        layer_norm_steps("A", x_in, 0, GB, (t.group_a + 1) * 3, True)
                    if k == 7 and s.following:
                        normalize("A", x_in, x_in, 0, GB, t.group_a + 2)
                    for op, r in s.tail if k == s.steps[-1] else []:
                        if op == "T":
                            turned(t, r)
                        if op == "V":
                            heads_low(t, r)
                        if op == "W":
                            add_residual(t, r)
                            apply_norm(t, r)

            run_pipeline(dve, shapes, body)

        @block.tensor
        def _(pe):
            pe.wait_ge(cols_loaded, 16 * (len(vectors) + len(rows) + 2))

            def shift_products(n, sources, bank, first, shift, chunks):
                for i, (w, kc) in enumerate(sources):
                    for m in range(w.shape[1] // P):
                        col = first(i, m, kc)
                        last = nc.tensor.matmul(p_bank[bank][:, col:col + 1], w[:, m * P:(m + 1) * P],
                                                cols[:, shift + kc:shift + kc + 1], start=True, stop=True)
                return last

            def bias_through_output(n, spread0, bank):
                for c in range(KC):
                    last = nc.tensor.matmul(p_bank[bank][:, 0:D], spread_bv[:, spread0 + c, :],
                                            staged[n % 2][:, W + c * D:W + (c + 1) * D], start=(c == 0),
                                            stop=(c == KC - 1))
                return last

            b1, b2 = at[L0 + "ln1_b"], at[L0 + "ln2_b"]
            for n in range(len(pieces)):
                pe.wait_ge(piece_loaded[n % 2], loaded_by[n])
                piece = staged[n % 2]
                part = lambda i: piece[:, i * D:(i + 1) * D]
                if n == 0:
                    shift_products(n, [(part(i), i % KC) for i in range(2 * KC)], 0,
                                   lambda i, m, kc: (i // KC) * KC * KC + m * KC + kc, b1, KC).then_inc(bias_products, 1)
                elif n == 1:
                    shift_products(n, [(part(i), i) for i in range(KC)], 0,
                                   lambda i, m, kc: 2 * KC * KC + m * KC + kc, b1, KC).then_inc(bias_products, 1)
                elif n == 2:
                    pe.wait_ge(bias_summed, 1)
                    bias_through_output(1, 0, 1)
                    shift_products(n, [(piece, 0)], 3, lambda i, m, kc: m, b2, FC).then_inc(bias_products, 1)
                elif n == 3:
                    shift_products(n, [(piece, 1)], 3, lambda i, m, kc: FC + m, b2, FC).then_inc(bias_products, 1)
                elif n == len(pieces) - 1:
                    bias_through_output(n, KC, 2).then_inc(bias_products, 1)
                else:
                    pe.nop().then_inc(bias_products, 1)
            setup_over(pe)

            def take(t, use):
                bank, number = t.bank(use)
                wait(pe, drained[bank], number - 1)
                return bank, p_bank[bank]

            def three_passes(dst, products, bias=None):
                n, total_n = 0, 3 * len(products) + (bias is not None)
                for stationary, moving in products:
                    for i, j in ((HI, HI), (HI, LO), (LO, HI)):
                        last = nc.tensor.matmul(dst, stationary(i), moving(j), start=(n == 0), stop=(n == total_n - 1))
                        n += 1
                if bias is not None:
                    last = nc.tensor.matmul(dst, pick[:, :], bias, start=False, stop=True)
                return last

            def work(t, op):
                kind, what = op
                for use in bank_uses(op):
                    bank, dst = take(t, use)
                    if kind == "XT":
                        c = use[2]
                        src = x_in if what == "A" else x_two
                        if c == 0 and what == "A":
                            pe.wait_ge(ln_applied["A"], t.group_a + 1)
                        if c == 0 and what == "M":
                            pe.wait_ge(ln_applied["M"], t.group_m + 1)
                        if c == 0 and what == "C":
                            for i in range(2):
                                b2_, n2_ = t.bank(("DOWN", i))
                                pe.wait_ge(drained[b2_], n2_)
                        for b in range(GB):
                            last = nc.tensor.transpose(dst[:, b * P:(b + 1) * P], src[:, b, c * P:(c + 1) * P], ident[:, :])
                    elif kind in "QK":
                        m = use[2]
                        w = weight[weights_of[what]["QK".index(kind)]]
                        wait_split(t, what)
                        last = three_passes(dst[:, :], [
                            (lambda i, kc=kc: w[:, i, kc, m * P:(m + 1) * P], lambda j, kc=kc: normed[:, j, kc, :])
                            for kc in range(KC)])
                    elif kind == "V":
                        w = weight[weights_of[what][2]]
                        for half_b in range(2):
                            b = 2 * use[2] + half_b
                            last = three_passes(dst[:, half_b * D:(half_b + 1) * D], [
                                (lambda i, kc=kc: normed[:, i, kc, b * P:(b + 1) * P], lambda j, kc=kc: w[:, j, kc, :])
                                for kc in range(KC)])
                    elif kind == "UP":
                        j0 = use[1]
                        wait_split(t, "M")
                        last = three_passes(dst[:, :], [
                            (lambda i, kc=kc: w_up[:, i, kc, j0 * P:(j0 + 1) * P], lambda j, kc=kc: normed[:, j, kc, :])
                            for kc in range(KC)])
                    elif kind == "DOWN":
                        for half_b in range(2):
                            b = 2 * what + half_b
                            products = [(lambda i, f=f: hidden[:, i, f, b * P:(b + 1) * P],
                                         lambda j, f=f: w_down[:, j, f, :]) for f in range(FC)]
                            if what == 0 and half_b == 0:
                                pe.wait_ge(hidden_made, (t.group_m + 1) * FC)
                            last = three_passes(dst[:, half_b * D:(half_b + 1) * D], products, bias_row["down"][:, :])
                    last.then_inc(filled[bank], 1)

            def wait_split(t, what):
                for c in range(KC):
                    bank, number = t.bank(("XT", what, c))
                    pe.wait_ge(drained[bank], number)

            def make_scores(t, k):
                s = t.s
                u, stage, b = t.unit(s.steps.index(k))
                if b == 0:
                    for i in range(KC):
                        bank, number = t.bank(("Q", stage, i), earlier=(stage == "C"))
                        pe.wait_ge(drained[bank], number)
                    pe.wait_ge(blocks_loaded[stage], (t.group(s.steps.index(k)) + 1) * HC * 16)
                for c in range(KC):
                    wait(pe, masked_made, u * H - H + HC * (c + 1))
                    moving = lambda j: key_blocks[:, j, c, :, b * P:(b + 1) * P]
                    three_passes(p_scores[:, c, :].rearrange("p (h n) -> p h n", h=HC),
                                 [(lambda i: queries[:, i, c, b * P:(b + 1) * P], moving)]).then_inc(scores_made, 1)

            def lagging(t, op, r):
                u, stage, b = t.unit(r)
                par = (r if r >= 0 else r + 8) % 2
                if op == "T":
                    for c in range(KC):
                        pe.wait_ge(probs_made, u * KC + c + 1)
                        wait(pe, turned_out0 if c == 0 else turned_out1, u)
                        for h in range(HC):
                            last = nc.tensor.transpose(p_probs[:, c, h * P:(h + 1) * P], scores[:, par, HC * c + h, :],
                                                       ident[:, :])
                        last.then_inc(probs_turned, 1)
                if op == "V":
                    bank, dst = take(t, ("O", r))
                    pe.wait_ge(turned_out0, u + 1)
                    pe.wait_ge(turned_out1, u + 1)
                    if b == 0:
                        for i in range(2):
                            bv_, nv_ = t.bank(("V", stage, i), earlier=(stage == "C"))
                            pe.wait_ge(drained[bv_], nv_)
                    for h in range(H):
                        j, c = h % HC, h // HC
                        last = nc.tensor.matmul(dst[HD * j:HD * (j + 1), c * P:(c + 1) * P],
                                                values[stage][:, b, h * HD:(h + 1) * HD], probs_t[:, h, :],
                                                start=True, stop=True)
                    last.then_inc(filled[bank], 1)
                if op == "W":
                    bank, number = t.bank_of_values(r)
                    pe.wait_ge(drained[bank], number)
                    bank, dst = take(t, ("W", r))
                    w = weight[weights_of[stage][3]]
                    three_passes(dst[:, 0:D], [(lambda i, c=c: heads_t[:, i, c, :], lambda j, c=c: w[:, j, c, :])
                                               for c in range(KC)], bias_row[bias_of[stage]][:, :]
                                 ).then_inc(filled[bank], 1)

            def body(t):
                s = t.s
                for k in range(STEPS):
                    if k in s.units:
                        make_scores(t, k)
                    for op in s.mid.get(k, []):
                        work(t, op)
                    for op, r in s.lag.get(k, []):
                        lagging(t, op, r)
                    for op in s.fill.get(k, []):
                        work(t, op)
                    for op, r in s.tail if k == s.steps[-1] else []:
                        lagging(t, op, r)

            run_pipeline(pe, shapes, body)


WEIGHTS = (["L0_gnn_" + n for n in ("ln1_g", "ln1_b", "ln2_g", "ln2_b", "wq", "bq", "wk", "bk", "wv", "bv",
                                    "wo", "bo", "w1", "b1", "w2", "b2")]
           + ["L1_gnn_" + n for n in ("Wq", "bq", "Wk", "bk", "Wv", "bv", "Wo", "bo", "gamma", "beta")])


def kernel(**inputs):
    import concourse.bacc as bacc
    from concourse.bass_utils import run_bass_kernel_spmd

    nc = bacc.Bacc("TRN2", target_bir_lowering=False, num_devices=1)
    arrays, tensors = {}, {}
    for name in ["x", "adj"] + WEIGHTS:
        a = np.ascontiguousarray(inputs[name])
        arrays["in_" + name] = a
        tensors[name] = nc.dram_tensor("in_" + name, a.shape, mybir.dt.from_np(a.dtype), kind="ExternalInput").ap()
    out = nc.dram_tensor("out", (B, P, D), F32, kind="ExternalOutput").ap()
    build(nc, tensors, out)
    results = run_bass_kernel_spmd(nc, [arrays], core_ids=[0])
    return results.results[0]["out"]
```

```python
from contextlib import ExitStack

import numpy as np

import concourse.bass as bass
from concourse import mybir

F32 = mybir.dt.float32
F32R = mybir.dt.float32r
I32 = mybir.dt.int32
ALU = mybir.AluOpType
ACT = mybir.ActivationFunctionType

P = 128
B = 128
D = 256
H = 8
HD = D // H
KC = D // P
HC = H // KC
FF = 4 * D
FC = FF // P
GB = 4
TOK = GB * P
NG = B // GB
STEPS = 8
EPS = 1e-5
MASKED = 3.0e38
LARGEST = 3.4e38
BANKS = 4
HI, LO = 0, 1



def lags(steps, pending, drain):
    t, w, v = ([-1], [-2, -1], [-1]) if pending else ([], [], [])
    by_step = {}
    for r, k in enumerate(steps):
        ops = []
        if t:
            ops.append(("T", t.pop(0)))
        if w and w[0] <= r - 2:
            ops.append(("W", w.pop(0)))
        if v:
            ops.append(("V", v.pop(0)))
        t.append(r)
        w.append(r)
        v.append(r)
        by_step[k] = ops
    last = len(steps) - 1
    tail = [("T", last), ("W", last - 1), ("V", last), ("W", last)] if drain else []
    return by_step, tail


class Shape:

    def __init__(self, it, stages, following, before, drain):
        self.it, self.following, self.before, self.drain = it, following, before, drain
        self.a, self.m, self.c = ("A" in stages), ("M" in stages), ("C" in stages)
        self.units = {k: ("C", k) for k in range(GB)} if self.c else {}
        if self.a:
            self.units.update({GB + k: ("A", k) for k in range(GB)})
        self.steps = sorted(self.units)
        self.order = [self.units[k] for k in self.steps]
        self.looped = it == "loop"
        self.turns = NG - 3 if self.looped else 1
        pending = before is not None and not before.drain
        self.lag, self.tail = lags(self.steps, pending, drain)
        self.late, waiting = {}, []
        for k in self.steps:
            self.late[k] = waiting
            waiting = [r for op, r in self.lag[k] if op == "W"]
        self.last = waiting + [r for op, r in self.tail if op == "W"] if drain else []
        a, m = self.a, self.m
        self.first = {0: [("XT", "A")] * a, 3: [("XT", "M")] * m, 5: [("XT", "C")] * m}
        self.fill = {0: [("K", "A")] * a, 1: [("V", "A")] * a, 2: [("Q", "A")] * a,
                     3: [("UP", None), ("DOWN", 0)] * m, 4: [("DOWN", 1)] * m,
                     5: [("K", "C")] * m, 6: [("Q", "C")] * m, 7: [("V", "C")] * m}
        self.use, self.high = {}, {}
        for k in range(STEPS):
            self.number(self.first.get(k, []), self.lag.get(k, []), self.fill.get(k, []))
            if k == self.steps[-1]:
                self.number([], self.tail, [])
        if before is None:
            self.unit0 = self.use0 = self.high0 = 0
        else:
            self.unit0 = before.unit0 + before.turns * len(before.order)
            self.use0 = before.use0 + before.turns * len(before.use)
            self.high0 = before.high0 + before.turns * len(before.high)
        assert not self.looped or len(self.use) % BANKS == 0

    def number(self, mid, lagging, fill):
        middle = [x for op in mid for x in bank_uses(op)]
        late = [("W" if o == "W" else "O", r) for o, r in lagging if o != "T"]
        final = [x for op in fill for x in bank_uses(op)]
        for x in middle + late + final:
            self.use[x] = len(self.use)
            if x[0] in ("XT", "Q", "K", "O"):
                self.high[x] = len(self.high)


def bank_uses(op):
    kind, what = op
    if kind == "UP":
        return [("UP", j) for j in range(FC)]
    if kind == "DOWN":
        return [("DOWN", what)]
    return [(kind, what, i) for i in range(2)]


def make_shapes():
    shapes, before = [], None
    for it, stages, following in [(0, "A", True), (1, "AM", True), ("loop", "AMC", True),
                                  (NG - 1, "AMC", False), (NG, "MC", False), (NG + 1, "C", False)]:
        before = Shape(it, stages, following, before, it in (0, NG, NG + 1))
        shapes.append(before)
    return shapes


class Turn:

    def __init__(self, shape, it):
        self.s, self.it = shape, it
        self.group_a, self.group_m, self.group_c = it, it - 1, it - 2

    def grown(self, base, each):
        return self.it * each + (base - 2 * each) if self.s.looped else base

    def unit(self, r):
        order = self.s.order if r >= 0 else self.s.before.order
        stage, b = order[r]
        return self.grown(self.s.unit0 + r, len(self.s.order)), stage, b

    def group(self, r):
        _, stage, _ = self.unit(r)
        return (self.group_a if stage == "A" else self.group_c) - (1 if r < 0 else 0)

    def bank(self, key, earlier=False):
        s = self.s
        n = s.use0 + (s.before.use[key] - len(s.before.use) if earlier else s.use[key])
        return n % BANKS, self.grown(n // BANKS + 1, len(s.use) // BANKS)

    def bank_of_values(self, r):
        if ("O", r) in self.s.use:
            return self.bank(("O", r))
        return self.bank(("O", len(self.s.before.order) + r), earlier=True)

    def high(self, key):
        return self.grown(self.s.high0 + self.s.high[key] + 1, len(self.s.high))


def run_pipeline(eng, shapes, body):
    for s in shapes:
        if s.looped:
            with eng.Fori(2, NG - 1) as it:
                body(Turn(s, it))
        else:
            body(Turn(s, s.it))


def wait(eng, sem, count):
    if not (isinstance(count, int) and count <= 0):
        eng.wait_ge(sem, count)


def build(nc, T, out):
    ctx = ExitStack()
    with ctx:
        def sb(name, shape, dt=F32):
            return ctx.enter_context(nc.sbuf_tensor(name, shape, dt))

        def sem(name):
            return ctx.enter_context(nc.semaphore(name))

        weight = {}
        for name in ("q0", "k0", "v0", "o0", "q1", "k1", "v1", "o1"):
            weight[name] = sb("w_" + name, [P, 2, KC, D], F32R)
        w_up = sb("w_up", [P, 2, KC, FF], F32R)
        w_down = sb("w_down", [P, 2, FC, D], F32R)
        bias_row = {n: sb("bias_" + n, [P, D], F32R) for n in ("o0", "down", "o1")}
        pick = sb("pick", [P, P], F32R)
        ident = sb("ident", [P, P])
        gamma, beta = sb("gamma", [P, D]), sb("beta", [P, D])
        cols = sb("cols", [P, 28])
        ready_cols = sb("ready_cols", [P, 16])
        half, fence, table_turn = sb("half", [P, GB]), sb("fence", [P, 16]), sb("table_turn", [P, 1])

        normed = sb("normed", [P, 2, KC, TOK], F32R)
        queries = {"A": sb("queries_a", [P, 2, KC, TOK], F32R), "C": sb("queries_c", [P, 2, KC, TOK], F32R)}
        key_blocks = sb("key_blocks", [P, KC, 2, HC, TOK], F32R)
        values = {"A": sb("values_a", [P, GB, D]), "C": sb("values_c", [P, GB, D])}
        scores = sb("scores", [P, 2, H, P])
        negmax, total, inverse = sb("negmax", [P, 2, H]), sb("total", [P, 2, H]), sb("inverse", [P, 2, H])
        probs_t = sb("probs_t", [P, H, P])
        heads_t = sb("heads_t", [P, 2, KC, P], F32R)
        hidden_raw = sb("hidden_raw", [P, 2, TOK])
        hidden = sb("hidden", [P, FC, 2, TOK], F32R)
        keys = hidden[:, FC - KC:FC, :, :]
        x_in = sb("x_in", [P, GB, D])
        res_a = sb("res_a", [P, GB, D])
        x_two = sb("x_two", [P, GB, D])
        res_c = sb("res_c", [P, GB, D])
        adj = {"A": sb("adj_a", [P, GB, P]), "C": sb("adj_c", [P, GB, P])}
        adj_tmp = sb("adj_tmp", [P, GB, P])
        stats = {n: sb("stats_" + n, [P, GB, 6]) for n in "AMC"}
        moments = {n: sb("moments_" + n, [P, GB, 2]) for n in "AMC"}
        spread = {n: sb("spread_" + n, [P, GB]) for n in "AMC"}
        rstd = {n: sb("rstd_" + n, [P, GB]) for n in "AMC"}

        p_scores = ctx.enter_context(nc.psum_tensor("p_scores", [P, KC, HC * P], F32))
        p_probs = ctx.enter_context(nc.psum_tensor("p_probs", [P, KC, HC * P], F32))
        p_bank = [ctx.enter_context(nc.psum_tensor(f"p_bank{i}", [P, TOK], F32)) for i in range(BANKS)]

        piece_loaded, cols_loaded = [sem("piece_loaded0"), sem("piece_loaded1")], sem("cols_loaded")
        consts_ready, piece_scaled, piece_high = sem("consts_ready"), sem("piece_scaled"), sem("piece_high")
        piece_done, bias_products, setup_vector = sem("piece_done"), sem("bias_products"), sem("setup_vector")
        zeroed, bias_summed = sem("zeroed"), sem("bias_summed")
        x_loaded, res_a_loaded, res_c_loaded = sem("x_loaded"), sem("res_a_loaded"), sem("res_c_loaded")
        adj_loaded = {"A": sem("adj_a_loaded"), "C": sem("adj_c_loaded")}
        blocks_loaded = {n: [sem(f"blocks_{n.lower()}_loaded{i}") for i in range(2)] for n in "AC"}
        stored = sem("stored")
        filled = [sem(f"filled{i}") for i in range(BANKS)]
        scores_made, probs_turned = sem("scores_made"), sem("probs_turned")
        drained = [sem(f"drained{i}") for i in range(BANKS)]
        high_made, exps_made, turned_out0 = sem("high_made"), sem("exps_made"), sem("turned_out0")
        masked_made, inverses_made, turned_out1 = sem("masked_made"), sem("inverses_made"), sem("turned_out1")
        hidden_high, hidden_made = sem("hidden_high"), sem("hidden_made")
        ln_steps = {n: sem("ln_steps_" + n) for n in "AMC"}
        ln_applied = {n: sem("ln_applied_" + n) for n in "AMC"}
        mask_steps = {"A": sem("mask_steps_a"), "C": sem("mask_steps_c")}
        probs_made, gained, finished = sem("probs_made"), sem("gained"), sem("finished")
        rstd_made = {n: sem("rstd_made_" + n) for n in "AMC"}

        x_view = T["x"].rearrange("b s d -> s b d")
        out_view = out.rearrange("b s d -> s b d")
        adj_view = T["adj"].rearrange("b q k -> q b k")

        def w_view(name):
            return T[name].rearrange("(c p) n -> p c n", p=P)

        L0, L1 = "L0_gnn_", "L1_gnn_"
        vectors = [(L0 + "ln1_g", KC), (L0 + "ln2_g", KC), (L0 + "ln1_b", KC), (L0 + "ln2_b", KC),
                   (L0 + "bq", KC), (L0 + "bk", KC), (L0 + "bv", KC), (L0 + "b1", FC),
                   (L1 + "bq", KC), (L1 + "bk", KC), (L1 + "bv", KC)]
        at, col = {}, 0
        for name, n in vectors:
            at[name] = col
            col += n
        assert col == cols.shape[1]
        rows = [("o0", L0 + "bo"), ("down", L0 + "b2"), ("o1", L1 + "bo")]
        QSCALE = -1.0 / float(np.sqrt(HD))

        W = KC * D
        flat = lambda t: t.rearrange("p c n -> p (c n)")
        whole = lambda name: (lambda part: flat(weight[name][:, part]))
        staged = [scores[:, i].rearrange("p h n -> p (h n)") for i in range(2)]
        scaled = probs_t[:, :, :].rearrange("p h n -> p (h n)")
        w1, w2 = w_view(L0 + "w1"), w_view(L0 + "w2")
        g1 = [cols[:, at[L0 + "ln1_g"] + c:at[L0 + "ln1_g"] + c + 1] for c in range(KC)]
        g2 = [cols[:, at[L0 + "ln2_g"] + c:at[L0 + "ln2_g"] + c + 1] for c in range(KC)]
        pieces = [
            ([w_view(L0 + "wq"), w_view(L0 + "wk")], [whole("q0"), whole("k0")],
             [(0, D, g1[0], QSCALE), (D, D, g1[1], QSCALE), (2 * D, D, g1[0], 1.0), (3 * D, D, g1[1], 1.0)]),
            ([w_view(L0 + "wv"), w_view(L0 + "wo")], [whole("v0"), whole("o0")],
             [(0, D, g1[0], 1.0), (D, D, g1[1], 1.0), (2 * D, 2 * D, 1.0, 1.0)]),
            ([w1[:, 0:1]], [lambda part: w_up[:, part, 0]], [(0, FF, g2[0], 1.0)]),
            ([w1[:, 1:2]], [lambda part: w_up[:, part, 1]], [(0, FF, g2[1], 1.0)]),
            ([w2[:, 0:4]], [lambda part: flat(w_down[:, part, 0:4])], [(0, FF, 1.0, 1.0)]),
            ([w2[:, 4:8]], [lambda part: flat(w_down[:, part, 4:8])], [(0, FF, 1.0, 1.0)]),
            ([w_view(L1 + "Wq"), w_view(L1 + "Wk")], [whole("q1"), whole("k1")],
             [(0, W, 1.0, QSCALE), (W, W, 1.0, 1.0)]),
            ([w_view(L1 + "Wv"), w_view(L1 + "Wo")], [whole("v1"), whole("o1")], [(0, 2 * W, 1.0, 1.0)]),
        ]
        loaded_by = [16 * sum(len(pieces[m][0]) for m in range(n % 2, n + 1, 2)) for n in range(len(pieces))]
        ZEROED = 8
        SETUP_VECTOR = 23
        spread_bv = adj_tmp
        row_raw = res_c

        def setup_over(eng):
            eng.wait_ge(piece_done, len(pieces))
            eng.wait_ge(setup_vector, SETUP_VECTOR)
            eng.wait_ge(zeroed, ZEROED)

        def copied(eng, t, before):
            stage = {"A": "C" if t.s.c else "A", "C": "A" if t.s.a else "C", "M": "A" if t.s.a else "C"}[before]
            group = t.group_c + 1 if stage == "C" else t.group_a if before == "A" else t.group_a + 1
            for blocks in blocks_loaded[stage]:
                wait(eng, blocks, group * HC * 16)

        def split_part(kind, stage, part, c):
            return queries[stage][:, part, c, :] if kind == "Q" else keys[:, c, part, :]

        shapes = make_shapes()
        weights_of = {"A": ("q0", "k0", "v0", "o0"), "C": ("q1", "k1", "v1", "o1")}
        residual = {"A": res_a, "C": res_c}
        bias_of = {"A": "o0", "C": "o1"}
        block = ctx.enter_context(nc.Block())

        @block.sync
        def _(sp):
            for name, n in vectors:
                sp.dma_start(cols[:, at[name]:at[name] + n], T[name].rearrange("(c p) -> p c", p=P),
                             allow_slow_non_contiguous=True).then_inc(cols_loaded, 16)
            for i, (_, name) in enumerate(rows):
                sp.dma_start(row_raw[:, i, :], T[name].partition_broadcast(P)).then_inc(cols_loaded, 16)
            sp.dma_start(gamma[:, :], T[L1 + "gamma"].partition_broadcast(P)).then_inc(cols_loaded, 16)
            sp.dma_start(beta[:, :], T[L1 + "beta"].partition_broadcast(P)).then_inc(cols_loaded, 16)
            for n, (loads, _, _) in enumerate(pieces):
                if n >= 2:
                    sp.wait_ge(piece_scaled, n - 1)
                    sp.wait_ge(bias_products, n)
                for i, src in enumerate(loads):
                    width = 2 * W // len(loads)
                    dst = staged[n % 2][:, i * width:(i + 1) * width].rearrange("p (c n) -> p c n", n=src.shape[2])
                    sp.dma_start(dst, src).then_inc(piece_loaded[n % 2], 16)
                if n == 1:
                    sp.dma_start(x_in[:, :, :], x_view[:, 0:GB, :]).then_inc(x_loaded, 16)
                    sp.dma_start(adj["A"][:, :, :].bitcast(I32), adj_view[:, 0:GB, :]).then_inc(adj_loaded["A"], 16)
            setup_over(sp)

            def drained_use(t, use):
                bank, number = t.bank(use)
                return drained[bank], number

            def load_blocks(stage, half, condition):
                sp.wait_ge(*condition)
                two = slice(half * TOK // 2, (half + 1) * TOK // 2)
                for j in range(HC):
                    rows_j = slice(HD * j, HD * (j + 1))
                    sp.dma_start(key_blocks[rows_j, :, :, j, two].bitcast(F32), keys[rows_j, :, :, two].bitcast(F32)
                                 ).then_inc(blocks_loaded[stage][half], 16)

            def store(t, b):
                sp.wait_ge(finished, t.group_c * GB + b + 1)
                sp.dma_start(out_view[:, bass.ds(t.group_c * GB + b, 1), :], res_c[:, b:b + 1, :]).then_inc(stored, 16)

            def body(t):
                s = t.s
                unit0 = t.grown(s.unit0, len(s.order))
                if s.a and s.following:
                    sp.wait_ge(*drained_use(t, ("XT", "A", 1)))
                    sp.dma_start(x_in[:, :, :], x_view[:, bass.ds((t.group_a + 1) * GB, GB), :]).then_inc(x_loaded, 16)
                if s.a:
                    last_use = (masked_made, (unit0 + 2) * H) if s.c else drained_use(t, ("K", "A", 1))
                    load_blocks("A", 0, last_use)
                    load_blocks("A", 1, (masked_made, (unit0 + GB) * H) if s.c else last_use)
                if s.c:
                    store(t, 0)
                    store(t, 1)
                if s.m:
                    if s.c:
                        sp.wait_ge(masked_made, (unit0 + GB) * H)
                    sp.dma_start(adj["C"][:, :, :].bitcast(I32), adj_view[:, bass.ds(t.group_m * GB, GB), :]
                                 ).then_inc(adj_loaded["C"], 16)
                if s.a:
                    if s.m:
                        sp.wait_ge(*drained_use(t, ("DOWN", 1)))
                    sp.dma_start(res_a[:, :, :], x_view[:, bass.ds(t.group_a * GB, GB), :]).then_inc(res_a_loaded, 16)
                if s.c:
                    store(t, 2)
                if s.m:
                    load_blocks("C", 0, drained_use(t, ("K", "C", 1)))
                if s.c:
                    store(t, 3)
                if s.m:
                    load_blocks("C", 1, (masked_made, (unit0 + len(s.order)) * H) if s.a
                                else drained_use(t, ("K", "C", 1)))
                    if s.c:
                        sp.wait_ge(stored, (t.group_c + 1) * GB * 16)
                    if not (s.a and s.c):
                        sp.wait_ge(*drained_use(t, ("DOWN", 1)))
                    sp.dma_start(res_c[:, :, :], x_two[:, :, :]).then_inc(res_c_loaded, 16)
                if s.a and s.following:
                    sp.wait_ge(masked_made, (unit0 + len(s.order)) * H)
                    sp.dma_start(adj["A"][:, :, :].bitcast(I32), adj_view[:, bass.ds((t.group_a + 1) * GB, GB), :]
                                 ).then_inc(adj_loaded["A"], 16)

            run_pipeline(sp, shapes, body)
            sp.wait_ge(stored, NG * GB * 16)

        @block.gpsimd
        def _(pool):
            nc.gpsimd.memset(ident[:, :], 0.0).then_inc(zeroed, 1)
            nc.gpsimd.memset(half[:, :], -0.5).then_inc(zeroed, 1)
            for t in bias_row.values():
                last = nc.gpsimd.memset(t[:, :].bitcast(F32), 0.0)
            last.then_inc(zeroed, 1)
            nc.gpsimd.memset(pick[:, :].bitcast(F32), 0.0).then_inc(zeroed, 1)
            pool.wait_ge(zeroed, 4)
            nc.gpsimd.affine_select(out=ident[:, :], in_=ident[:, :], compare_op=ALU.not_equal, fill=1.0,
                                    base=0, pattern=[[-1, P]], channel_multiplier=1).then_inc(zeroed, 1)
            pool.wait_ge(zeroed, 5)
            nc.gpsimd.memset(pick[0:1, :].bitcast(F32), 1.0).then_inc(zeroed, 1)
            pool.wait_ge(zeroed, 6)
            nc.gpsimd.memset(pick[32:33, :].bitcast(F32), 1.0).then_inc(zeroed, 1)
            pool.wait_ge(zeroed, 7)
            nc.gpsimd.memset(key_blocks[:, :, :, :, :].bitcast(F32), 0.0).then_inc(zeroed, 1)

            def make_rstd(n, b0, b1, steps):
                pool.wait_ge(ln_steps[n], steps)
                nc.gpsimd.tensor_tensor(rstd[n][:, b0:b1], spread[n][:, b0:b1], half[:, b0:b1], ALU.pow
                                        ).then_inc(rstd_made[n], 1)

            make_rstd("A", 0, GB, 3)
            setup_over(pool)

            def rstd_of(t, ops):
                for op, r in ops:
                    if op == "W":
                        _, stage, b = t.unit(r)
                        if stage == "A" and b == GB - 1:
                            make_rstd("M", 0, GB, t.group(r) * 3 + 3)
                        if stage == "C":
                            make_rstd("C", b, b + 1, (t.group(r) * GB + b) * 3 + 3)

            def finish(t, r):
                _, stage, b = t.unit(r)
                if stage == "C":
                    unit = t.group(r) * GB + b
                    pool.wait_ge(ln_applied["C"], unit + 1)
                    nc.gpsimd.tensor_tensor(res_c[:, b], res_c[:, b], gamma[:, :], ALU.mult).then_inc(gained, 1)
                    pool.wait_ge(gained, unit + 1)
                    nc.gpsimd.tensor_tensor(res_c[:, b], res_c[:, b], beta[:, :], ALU.add).then_inc(finished, 1)

            def body(t):
                s = t.s
                for k in range(STEPS):
                    for c in range(KC) if k in s.units else []:
                        u, _, _ = t.unit(s.steps.index(k))
                        pool.wait_ge(inverses_made, u * KC + c + 1)
                        heads = slice(HC * c, HC * (c + 1))
                        rows_c = scores[:, k % 2, heads, :]
                        nc.gpsimd.tensor_tensor(
                            rows_c, rows_c, inverse[:, k % 2, heads].unsqueeze(2).broadcast_to([P, HC, P]),
                            ALU.mult).then_inc(probs_made, 1)
                    for r in s.late.get(k, []):
                        finish(t, r)
                    rstd_of(t, s.lag.get(k, []))
                    if k == 3 and s.following:
                        make_rstd("A", 0, GB, (t.group_a + 1) * 3 + 3)
                    if k == s.steps[-1]:
                        rstd_of(t, s.tail)
                        for r in s.last:
                            finish(t, r)

            run_pipeline(pool, shapes, body)

        @block.scalar
        def _(act):
            for n, (_, targets, _) in enumerate(pieces):
                act.wait_ge(piece_scaled, n + 1)
                width = 2 * W // len(targets)
                for i, target in enumerate(targets):
                    last = nc.scalar.activation(target(HI), scaled[:, i * width:(i + 1) * width], ACT.Copy)
                last.then_inc(piece_high, 1)
            setup_over(act)

            def exps(t, k, c):
                u, _, _ = t.unit(t.s.steps.index(k))
                for h in range(HC * c, HC * (c + 1)):
                    if h % 2 == 0:
                        act.wait_ge(masked_made, u * H + h + 2)
                    last = nc.scalar.activation(scores[:, k % 2, h], scores[:, k % 2, h], ACT.Exp, scale=-1.0,
                                                bias=negmax[:, k % 2, h:h + 1], accum_out=total[:, k % 2, h:h + 1])
                last.then_inc(exps_made, 1)

            def evacuate(t, op):
                kind, what = op
                for use in bank_uses(op):
                    bank, number = t.bank(use)
                    src = p_bank[bank]
                    act.wait_ge(filled[bank], number)
                    if kind == "XT":
                        nc.scalar.activation(normed[:, HI, use[2], :], src[:, :], ACT.Copy).then_inc(high_made, 1)
                    elif kind in "QK":
                        if kind == "K":
                            copied(act, t, what)
                        bias = 4 * (what == "C") + 2 * (kind == "K") + use[2]
                        nc.scalar.activation(split_part(kind, what, HI, use[2]), src[:, :], ACT.Identity,
                                             bias=ready_cols[:, bias:bias + 1]).then_inc(high_made, 1)
                    elif kind == "V":
                        dst = values[what][:, 2 * use[2]:2 * use[2] + 2, :].rearrange("p g n -> p (g n)")
                        nc.scalar.activation(dst, src[:, :], ACT.Copy).then_inc(drained[bank], 1)
                    elif kind == "UP":
                        j = use[1]
                        wait(act, hidden_made, t.group_m * FC + j - 1)
                        nc.scalar.activation(hidden_raw[:, j % 2], src[:, :], ACT.Gelu,
                                             bias=ready_cols[:, 8 + j:9 + j]).then_inc(drained[bank], 1)

            def turned(t, r):
                u, _, _ = t.unit(r)
                act.wait_ge(probs_turned, u * KC + 1)
                nc.scalar.activation(probs_t[:, 0:HC].rearrange("p h n -> p (h n)"), p_probs[:, 0, :], ACT.Copy
                                     ).then_inc(turned_out0, 1)

            def heads_high(t, r):
                bank, number = t.bank(("O", r))
                act.wait_ge(filled[bank], number)
                nc.scalar.activation(heads_t[:, HI].rearrange("p c n -> p (c n)"), p_bank[bank][:, 0:KC * P],
                                     ACT.Copy).then_inc(high_made, 1)

            def body(t):
                s = t.s
                for k in range(STEPS):
                    lag = s.lag.get(k, [])
                    for op in s.first.get(k, []):
                        evacuate(t, op)
                    for op, r in lag:
                        if op == "T":
                            turned(t, r)
                    if k in s.units:
                        exps(t, k, 0)
                    for op, r in lag:
                        if op == "V":
                            heads_high(t, r)
                    if k in s.units:
                        exps(t, k, 1)
                    for op in s.fill.get(k, []):
                        if op[0] != "DOWN":
                            evacuate(t, op)
                        if op[0] == "UP":
                            nc.scalar.activation(table_turn[:, :], half[:, 0:1], ACT.Exp)
                    for op, r in s.tail if k == s.steps[-1] else []:
                        if op == "T":
                            turned(t, r)
                        if op == "V":
                            heads_high(t, r)

            run_pipeline(act, shapes, body)

        @block.vector
        def _(dve):
            step, taken = [0], [0]

            def then(instruction):
                step[0] += 1
                instruction.then_inc(setup_vector, 1)
                dve.wait_ge(setup_vector, step[0])

            def take_wait():
                at_col = taken[0] % fence.shape[1]
                taken[0] += 1
                nc.vector.memset(fence[:, at_col:at_col + 1], 0.0)

            def layer_norm_steps(n, src, b0, b1, done, measure):
                if measure:
                    for b in range(b0, b1):
                        last = nc.vector.bn_stats(stats[n][:, b, :], src[:, b, :])
                    last.then_inc(ln_steps[n], 1)
                dve.wait_ge(ln_steps[n], done + 1)
                take_wait()
                for b in range(b0, b1):
                    last = nc.vector.bn_aggr(moments[n][:, b, :], stats[n][:, b, :])
                last.then_inc(ln_steps[n], 1)
                dve.wait_ge(ln_steps[n], done + 2)
                nc.vector.tensor_scalar(spread[n][:, b0:b1], moments[n][:, b0:b1, 1], EPS, None, ALU.add
                                        ).then_inc(ln_steps[n], 1)

            def normalize(n, src, dst, b0, b1, made):
                dve.wait_ge(rstd_made[n], made)
                for b in range(b0, b1):
                    last = nc.vector.tensor_scalar(dst[:, b, :], src[:, b, :], moments[n][:, b, 0:1],
                                                   rstd[n][:, b:b + 1], ALU.subtract, ALU.mult)
                last.then_inc(ln_applied[n], 1)

            def mask_a(group):
                a = adj["A"][:, :, :]
                dve.wait_ge(adj_loaded["A"], (group + 1) * 16)
                nc.vector.scalar_tensor_tensor(out=adj_tmp[:, :, :], in0=a.bitcast(I32), scalar=-0.1,
                                               in1=a.bitcast(I32), op0=ALU.mult, op1=ALU.mult
                                               ).then_inc(mask_steps["A"], 1)
                dve.wait_ge(mask_steps["A"], group * 3 + 1)
                nc.vector.tensor_scalar(a, a.bitcast(I32), 0.0, MASKED, ALU.is_le, ALU.mult
                                        ).then_inc(mask_steps["A"], 1)
                dve.wait_ge(mask_steps["A"], group * 3 + 2)
                nc.vector.tensor_tensor(a, a, adj_tmp[:, :, :], ALU.add).then_inc(mask_steps["A"], 1)
                dve.wait_ge(mask_steps["A"], group * 3 + 3)

            def mask_c(group):
                a = adj["C"][:, :, :]
                dve.wait_ge(adj_loaded["C"], (group + 1) * 16)
                nc.vector.tensor_scalar(a, a.bitcast(I32), 0.0, MASKED, ALU.is_equal, ALU.mult
                                        ).then_inc(mask_steps["C"], 1)
                dve.wait_ge(mask_steps["C"], group + 1)

            dve.wait_ge(cols_loaded, 16 * (len(vectors) + len(rows) + 2))
            dve.wait_ge(zeroed, ZEROED - 1)

            def bias_rows(i, name, psum):
                t = row_raw[:, i, :]
                if psum is not None:
                    then(nc.vector.tensor_tensor(t, psum, t, ALU.add))
                nc.vector.tensor_copy(bias_row[name][0:1, :], t[0:1, :])
                then(nc.vector.tensor_copy(bias_row[name][32:33, :], t[32:33, :]))
                then(nc.vector.tensor_tensor(bias_row[name][32:33, :], t[32:33, :],
                                             bias_row[name][32:33, :].bitcast(F32), ALU.subtract))

            then(nc.vector.memset(spread_bv[:, :, :], 1.0))
            for c in range(KC):
                q, bk, bv = at[L1 + "bq"] + c, at[L1 + "bk"] + c, at[L1 + "bv"] + c
                then(nc.vector.tensor_scalar(ready_cols[:, 4 + c:5 + c], cols[:, q:q + 1], QSCALE, None, ALU.mult))
                then(nc.vector.tensor_copy(ready_cols[:, 6 + c:7 + c], cols[:, bk:bk + 1]))
                then(nc.vector.tensor_scalar(spread_bv[:, KC + c, :], spread_bv[:, KC + c, :], cols[:, bv:bv + 1],
                                             None, ALU.mult))
            bias_rows(1, "down", None)
            biases = cols[:, at[L0 + "bq"]:at[L0 + "bq"] + 3 * KC]
            up_bias = cols[:, at[L0 + "b1"]:at[L0 + "b1"] + FC]
            for n, (_, targets, factors) in enumerate(pieces):
                dve.wait_ge(piece_loaded[n % 2], loaded_by[n])
                if n:
                    dve.wait_ge(piece_high, n)
                    dve.wait_ge(piece_done, n)
                for start, width, gain, factor in factors:
                    last = nc.vector.tensor_scalar(scaled[:, start:start + width], staged[n % 2][:, start:start + width],
                                                   gain, factor, ALU.mult, ALU.mult)
                last.then_inc(piece_scaled, 1)
                dve.wait_ge(piece_high, n + 1)
                width = 2 * W // len(targets)
                for i, target in enumerate(targets):
                    last = nc.vector.tensor_tensor(target(LO), scaled[:, i * width:(i + 1) * width],
                                                   target(HI).bitcast(F32), ALU.subtract)
                last.then_inc(piece_done, 1)
                if n == 1:
                    dve.wait_ge(bias_products, 2)
                    sums = p_bank[0][:, 0:3 * KC * KC].rearrange("p (x c) -> p c x", c=KC)
                    then(nc.vector.tensor_tensor(biases, sums[:, 0], biases, ALU.add))
                    then(nc.vector.tensor_tensor(biases, sums[:, 1], biases, ALU.add))
                    then(nc.vector.tensor_scalar(ready_cols[:, 0:2], biases[:, 0:2], QSCALE, None, ALU.mult))
                    then(nc.vector.tensor_copy(ready_cols[:, 2:4], biases[:, 2:4]))
                    for c in range(KC):
                        then(nc.vector.tensor_scalar(spread_bv[:, c, :], spread_bv[:, c, :], biases[:, 4 + c:5 + c],
                                                     None, ALU.mult))
                    nc.vector.memset(spread["C"][:, :], 1.0).then_inc(bias_summed, 1)
                if n == 2:
                    dve.wait_ge(bias_products, 3)
                    bias_rows(0, "o0", p_bank[1][:, 0:D])
                if n == 3:
                    dve.wait_ge(bias_products, 4)
                    sums = p_bank[3][:, 0:FC * KC].rearrange("p (c x) -> p c x", c=KC)
                    then(nc.vector.tensor_tensor(up_bias, sums[:, 0], up_bias, ALU.add))
                    then(nc.vector.tensor_tensor(ready_cols[:, 8:16], sums[:, 1], up_bias, ALU.add))
            dve.wait_ge(bias_products, len(pieces))
            bias_rows(2, "o1", p_bank[2][:, 0:D])
            assert step[0] == SETUP_VECTOR, step[0]
            dve.wait_ge(x_loaded, 16)
            layer_norm_steps("A", x_in, 0, GB, 0, True)
            normalize("A", x_in, x_in, 0, GB, 1)
            mask_a(0)
            setup_over(dve)

            def mask_scores(t, k, c):
                u, stage, b = t.unit(t.s.steps.index(k))
                dve.wait_ge(scores_made, u * KC + c + 1)
                take_wait()
                for h in range(HC * c, HC * (c + 1)):
                    nc.vector.tensor_tensor_reduce(
                        out=scores[:, k % 2, h], in0=p_scores[:, c, (h % HC) * P:(h % HC + 1) * P],
                        in1=adj[stage][:, b, :], scale=1.0, scalar=LARGEST, op0=ALU.add, op1=ALU.min,
                        accum_out=negmax[:, k % 2, h:h + 1]).then_inc(masked_made, 1)

            def invert(t, k, c):
                u, _, _ = t.unit(t.s.steps.index(k))
                dve.wait_ge(exps_made, u * KC + c + 1)
                heads = slice(HC * c, HC * (c + 1))
                nc.vector.reciprocal(inverse[:, k % 2, heads], total[:, k % 2, heads]).then_inc(inverses_made, 1)

            def evacuate(t, op):
                kind, what = op
                for use in bank_uses(op):
                    bank, number = t.bank(use)
                    src = p_bank[bank]
                    if kind == "XT":
                        dve.wait_ge(high_made, t.high(use))
                        hi, lo = normed[:, HI, use[2], :], normed[:, LO, use[2], :]
                        nc.vector.tensor_tensor(lo, src[:, :], hi.bitcast(F32), ALU.subtract).then_inc(drained[bank], 1)
                    elif kind in "QK":
                        dve.wait_ge(high_made, t.high(use))
                        bias = 4 * (what == "C") + 2 * (kind == "K") + use[2]
                        nc.vector.scalar_tensor_tensor(
                            out=split_part(kind, what, LO, use[2]), in0=src[:, :], scalar=ready_cols[:, bias:bias + 1],
                            in1=split_part(kind, what, HI, use[2]).bitcast(F32), op0=ALU.add, op1=ALU.subtract
                        ).then_inc(drained[bank], 1)
                    elif kind == "UP":
                        j = use[1]
                        if j == FC - KC:
                            copied(dve, t, "M")
                        dve.wait_ge(drained[bank], number)
                        nc.vector.tensor_copy(hidden[:, j, HI, :], hidden_raw[:, j % 2]).then_inc(hidden_high, 1)
                        dve.wait_ge(hidden_high, t.group_m * FC + j + 1)
                        nc.vector.tensor_tensor(hidden[:, j, LO, :], hidden_raw[:, j % 2],
                                                hidden[:, j, HI, :].bitcast(F32), ALU.subtract
                                                ).then_inc(hidden_made, 1)
                    elif kind == "DOWN":
                        dve.wait_ge(filled[bank], number)
                        two = slice(2 * what, 2 * what + 2)
                        both = lambda x: x[:, two, :].rearrange("p g n -> p (g n)")
                        nc.vector.tensor_tensor(both(x_two), src[:, :], both(res_a), ALU.add
                                                ).then_inc(drained[bank], 1)

            def turned(t, r):
                u, _, _ = t.unit(r)
                dve.wait_ge(probs_turned, u * KC + 2)
                nc.vector.tensor_copy(probs_t[:, HC:H].rearrange("p h n -> p (h n)"), p_probs[:, 1, :]
                                      ).then_inc(turned_out1, 1)

            def heads_low(t, r):
                bank, _ = t.bank(("O", r))
                dve.wait_ge(high_made, t.high(("O", r)))
                part = lambda i: heads_t[:, i].rearrange("p c n -> p (c n)")
                nc.vector.tensor_tensor(part(LO), p_bank[bank][:, 0:KC * P], part(HI).bitcast(F32), ALU.subtract
                                        ).then_inc(drained[bank], 1)

            def add_residual(t, r):
                _, stage, b = t.unit(r)
                group = t.group(r)
                bank, number = t.bank(("W", r))
                dve.wait_ge(filled[bank], number)
                dve.wait_ge(res_a_loaded if stage == "A" else res_c_loaded, (group + 1) * 16)
                x = residual[stage]
                nc.vector.tensor_tensor(x[:, b, :], p_bank[bank][:, 0:D], x[:, b, :], ALU.add
                                        ).then_inc(drained[bank], 1)
                dve.wait_ge(drained[bank], number)
                if stage == "C":
                    layer_norm_steps("C", x, b, b + 1, (group * GB + b) * 3, True)
                else:
                    last = nc.vector.bn_stats(stats["M"][:, b, :], x[:, b, :])
                    if b == GB - 1:
                        last.then_inc(ln_steps["M"], 1)
                        layer_norm_steps("M", x, 0, GB, group * 3, False)

            def apply_norm(t, r):
                _, stage, b = t.unit(r)
                group = t.group(r)
                if stage == "C":
                    normalize("C", res_c, res_c, b, b + 1, group * GB + b + 1)
                elif b == GB - 1:
                    wait(dve, res_c_loaded, group * 16)
                    normalize("M", res_a, x_two, 0, GB, group + 1)

            def prepare(t, k):
                s = t.s
                if k == 3 and s.a and s.before is not None:
                    mask_a(t.group_a)
                if k == 3 and s.following:
                    dve.wait_ge(x_loaded, (t.group_a + 2) * 16)
                    layer_norm_steps("A", x_in, 0, GB, (t.group_a + 1) * 3, True)
                if k == 4 and s.following:
                    normalize("A", x_in, x_in, 0, GB, t.group_a + 2)
                if k == 4 and s.m:
                    mask_c(t.group_m)

            def body(t):
                s = t.s
                for k in range(STEPS):
                    lag = s.lag.get(k, [])
                    for op in s.first.get(k, []):
                        evacuate(t, op)
                    if k in s.units:
                        mask_scores(t, k, 0)
                    for op, r in lag:
                        if op == "T":
                            turned(t, r)
                    if k in s.units:
                        mask_scores(t, k, 1)
                        invert(t, k, 0)
                    for r in s.late.get(k, []):
                        apply_norm(t, r)
                    for op, r in lag:
                        if op == "W":
                            add_residual(t, r)
                        if op == "V":
                            heads_low(t, r)
                    if k in s.units:
                        invert(t, k, 1)
                    fill = s.fill.get(k, [])
                    for op in fill:
                        if op[0] == "DOWN":
                            prepare(t, k)
                        evacuate(t, op)
                    if not s.m:
                        prepare(t, k)
                    for op, r in s.tail if k == s.steps[-1] else []:
                        if op == "T":
                            turned(t, r)
                        if op == "V":
                            heads_low(t, r)
                        if op == "W":
                            add_residual(t, r)
                    for r in s.last if k == s.steps[-1] else []:
                        apply_norm(t, r)

            run_pipeline(dve, shapes, body)

        @block.tensor
        def _(pe):
            pe.wait_ge(cols_loaded, 16 * (len(vectors) + len(rows) + 2))

            def shift_products(n, sources, bank, first, shift, chunks):
                for i, (w, kc) in enumerate(sources):
                    for m in range(w.shape[1] // P):
                        col = first(i, m, kc)
                        last = nc.tensor.matmul(p_bank[bank][:, col:col + 1], w[:, m * P:(m + 1) * P],
                                                cols[:, shift + kc:shift + kc + 1], start=True, stop=True)
                return last

            def bias_through_output(n, spread0, bank):
                for c in range(KC):
                    last = nc.tensor.matmul(p_bank[bank][:, 0:D], spread_bv[:, spread0 + c, :],
                                            staged[n % 2][:, W + c * D:W + (c + 1) * D], start=(c == 0),
                                            stop=(c == KC - 1))
                return last

            b1, b2 = at[L0 + "ln1_b"], at[L0 + "ln2_b"]
            for n in range(len(pieces)):
                pe.wait_ge(piece_loaded[n % 2], loaded_by[n])
                piece = staged[n % 2]
                part = lambda i: piece[:, i * D:(i + 1) * D]
                if n == 0:
                    shift_products(n, [(part(i), i % KC) for i in range(2 * KC)], 0,
                                   lambda i, m, kc: (i // KC) * KC * KC + m * KC + kc, b1, KC).then_inc(bias_products, 1)
                elif n == 1:
                    shift_products(n, [(part(i), i) for i in range(KC)], 0,
                                   lambda i, m, kc: 2 * KC * KC + m * KC + kc, b1, KC).then_inc(bias_products, 1)
                elif n == 2:
                    pe.wait_ge(bias_summed, 1)
                    bias_through_output(1, 0, 1)
                    shift_products(n, [(piece, 0)], 3, lambda i, m, kc: m, b2, FC).then_inc(bias_products, 1)
                elif n == 3:
                    shift_products(n, [(piece, 1)], 3, lambda i, m, kc: FC + m, b2, FC).then_inc(bias_products, 1)
                elif n == len(pieces) - 1:
                    bias_through_output(n, KC, 2).then_inc(bias_products, 1)
                else:
                    pe.nop().then_inc(bias_products, 1)
            setup_over(pe)

            def take(t, use):
                bank, number = t.bank(use)
                wait(pe, drained[bank], number - 1)
                return bank, p_bank[bank]

            def three_passes(dst, products, bias=None, chunks=None):
                n, total_n = 0, 3 * len(products) + (bias is not None)
                for f, (stationary, moving) in enumerate(products):
                    if chunks is not None:
                        pe.wait_ge(hidden_made, chunks + f + 1)
                    for i, j in ((HI, HI), (HI, LO), (LO, HI)):
                        last = nc.tensor.matmul(dst, stationary(i), moving(j), start=(n == 0), stop=(n == total_n - 1))
                        n += 1
                if bias is not None:
                    last = nc.tensor.matmul(dst, pick[:, :], bias, start=False, stop=True)
                return last

            def work(t, op):
                kind, what = op
                if kind == "XT":
                    src = x_in if what == "A" else x_two
                    if what != "C":
                        group = t.group_a if what == "A" else t.group_m
                        pe.wait_ge(ln_applied[what], group + 1)
                    for i in range(2):
                        if what == "C":
                            bank, number = t.bank(("DOWN", i))
                            pe.wait_ge(drained[bank], number)
                        for c, use in enumerate(bank_uses(op)):
                            bank, dst = take(t, use) if i == 0 else (t.bank(use)[0], p_bank[t.bank(use)[0]])
                            for b in range(2 * i, 2 * i + 2):
                                last = nc.tensor.transpose(dst[:, b * P:(b + 1) * P], src[:, b, c * P:(c + 1) * P],
                                                           ident[:, :])
                            if i == 1:
                                last.then_inc(filled[bank], 1)
                    return
                for use in bank_uses(op):
                    bank, dst = take(t, use)
                    if kind in "QK":
                        m = use[2]
                        w = weight[weights_of[what]["QK".index(kind)]]
                        wait_split(t, what)
                        last = three_passes(dst[:, :], [
                            (lambda i, kc=kc: w[:, i, kc, m * P:(m + 1) * P], lambda j, kc=kc: normed[:, j, kc, :])
                            for kc in range(KC)])
                    elif kind == "V":
                        w = weight[weights_of[what][2]]
                        for half_b in range(2):
                            b = 2 * use[2] + half_b
                            last = three_passes(dst[:, half_b * D:(half_b + 1) * D], [
                                (lambda i, kc=kc: normed[:, i, kc, b * P:(b + 1) * P], lambda j, kc=kc: w[:, j, kc, :])
                                for kc in range(KC)])
                    elif kind == "UP":
                        j0 = use[1]
                        wait_split(t, "M")
                        last = three_passes(dst[:, :], [
                            (lambda i, kc=kc: w_up[:, i, kc, j0 * P:(j0 + 1) * P], lambda j, kc=kc: normed[:, j, kc, :])
                            for kc in range(KC)])
                    elif kind == "DOWN":
                        for half_b in range(2):
                            b = 2 * what + half_b
                            products = [(lambda i, f=f: hidden[:, f, i, b * P:(b + 1) * P],
                                         lambda j, f=f: w_down[:, j, f, :]) for f in range(FC)]
                            chunks = t.group_m * FC if what == 0 and half_b == 0 else None
                            last = three_passes(dst[:, half_b * D:(half_b + 1) * D], products,
                                                bias_row["down"][:, :], chunks)
                    last.then_inc(filled[bank], 1)

            def wait_split(t, what):
                for c in range(KC):
                    bank, number = t.bank(("XT", what, c))
                    pe.wait_ge(drained[bank], number)

            def make_scores(t, k):
                s = t.s
                u, stage, b = t.unit(s.steps.index(k))
                if b == 0:
                    for i in range(KC):
                        bank, number = t.bank(("Q", stage, i), earlier=(stage == "C"))
                        pe.wait_ge(drained[bank], number)
                if b % 2 == 0:
                    pe.wait_ge(blocks_loaded[stage][b // 2], (t.group(s.steps.index(k)) + 1) * HC * 16)
                for c in range(KC):
                    wait(pe, masked_made, u * H - H + HC * (c + 1))
                    moving = lambda j: key_blocks[:, c, j, :, b * P:(b + 1) * P]
                    three_passes(p_scores[:, c, :].rearrange("p (h n) -> p h n", h=HC),
                                 [(lambda i: queries[stage][:, i, c, b * P:(b + 1) * P], moving)]).then_inc(scores_made, 1)

            def lagging(t, op, r):
                u, stage, b = t.unit(r)
                par = (r if r >= 0 else r + 8) % 2
                if op == "T":
                    for c in range(KC):
                        pe.wait_ge(probs_made, u * KC + c + 1)
                        wait(pe, turned_out0 if c == 0 else turned_out1, u)
                        for h in range(HC):
                            last = nc.tensor.transpose(p_probs[:, c, h * P:(h + 1) * P], scores[:, par, HC * c + h, :],
                                                       ident[:, :])
                        last.then_inc(probs_turned, 1)
                if op == "V":
                    bank, dst = take(t, ("O", r))
                    pe.wait_ge(turned_out0, u + 1)
                    pe.wait_ge(turned_out1, u + 1)
                    if b == 0:
                        for i in range(2):
                            bv_, nv_ = t.bank(("V", stage, i), earlier=(stage == "C"))
                            pe.wait_ge(drained[bv_], nv_)
                    for h in range(H):
                        j, c = h % HC, h // HC
                        last = nc.tensor.matmul(dst[HD * j:HD * (j + 1), c * P:(c + 1) * P],
                                                values[stage][:, b, h * HD:(h + 1) * HD], probs_t[:, h, :],
                                                start=True, stop=True)
                    last.then_inc(filled[bank], 1)
                if op == "W":
                    bank, number = t.bank_of_values(r)
                    pe.wait_ge(drained[bank], number)
                    bank, dst = take(t, ("W", r))
                    w = weight[weights_of[stage][3]]
                    three_passes(dst[:, 0:D], [(lambda i, c=c: heads_t[:, i, c, :], lambda j, c=c: w[:, j, c, :])
                                               for c in range(KC)], bias_row[bias_of[stage]][:, :]
                                 ).then_inc(filled[bank], 1)

            def body(t):
                s = t.s
                for k in range(STEPS):
                    for op in s.first.get(k, []):
                        work(t, op)
                    if k in s.units:
                        make_scores(t, k)
                    for op, r in s.lag.get(k, []):
                        lagging(t, op, r)
                    for op in s.fill.get(k, []):
                        work(t, op)
                    for op, r in s.tail if k == s.steps[-1] else []:
                        lagging(t, op, r)

            run_pipeline(pe, shapes, body)


WEIGHTS = (["L0_gnn_" + n for n in ("ln1_g", "ln1_b", "ln2_g", "ln2_b", "wq", "bq", "wk", "bk", "wv", "bv",
                                    "wo", "bo", "w1", "b1", "w2", "b2")]
           + ["L1_gnn_" + n for n in ("Wq", "bq", "Wk", "bk", "Wv", "bv", "Wo", "bo", "gamma", "beta")])


def kernel(**inputs):
    import concourse.bacc as bacc
    from concourse.bass_utils import run_bass_kernel_spmd

    nc = bacc.Bacc("TRN2", target_bir_lowering=False, num_devices=1)
    arrays, tensors = {}, {}
    for name in ["x", "adj"] + WEIGHTS:
        a = np.ascontiguousarray(inputs[name])
        arrays["in_" + name] = a
        tensors[name] = nc.dram_tensor("in_" + name, a.shape, mybir.dt.from_np(a.dtype), kind="ExternalInput").ap()
    out = nc.dram_tensor("out", (B, P, D), F32, kind="ExternalOutput").ap()
    build(nc, tensors, out)
    results = run_bass_kernel_spmd(nc, [arrays], core_ids=[0])
    return results.results[0]["out"]
```

```python
from contextlib import ExitStack

import numpy as np

import concourse.bass as bass
from concourse import mybir

F32 = mybir.dt.float32
F32R = mybir.dt.float32r
I32 = mybir.dt.int32
ALU = mybir.AluOpType
ACT = mybir.ActivationFunctionType

P = 128
B = 128
D = 256
H = 8
HD = D // H
KC = D // P
HC = H // KC
FF = 4 * D
FC = FF // P
GB = 4
TOK = GB * P
NG = B // GB
STEPS = 8
EPS = 1e-5
MASKED = 3.0e38
LARGEST = 3.4e38
BANKS = 4
EARLY_PIECES = 2
PIECE_STEPS = {0: [2], 1: [3], 3: [4], 4: [5], 5: [6], 6: [7]}
BIAS_STEPS = {0: 1, 1: 2, 2: 3, 7: 7}
HI, LO = 0, 1


def lags(steps, pending, drain):
    by_step = {}
    for r, k in enumerate(steps):
        by_step[k] = ([("V", r - 2), ("W", r - 2)] if r >= 2 or pending else []) + (
            [("T", r - 1)] if r >= 1 or pending else [])
    last = len(steps) - 1
    tail = [("V", last - 1), ("T", last), ("W", last - 1), ("V", last), ("W", last)] if drain else []
    return by_step, tail


class Shape:

    def __init__(self, it, stages, following, before, drain):
        self.it, self.following, self.before, self.drain = it, following, before, drain
        self.a, self.m, self.c = ("A" in stages), ("M" in stages), ("C" in stages)
        self.units = {k: ("C", k) for k in range(GB)} if self.c else {}
        if self.a:
            self.units.update({GB + k: ("A", k) for k in range(GB)})
        self.steps = sorted(self.units)
        self.order = [self.units[k] for k in self.steps]
        self.looped = it == "loop"
        self.turns = NG - 3 if self.looped else 1
        pending = before is not None and not before.drain
        self.lag, self.tail = lags(self.steps, pending, drain)
        self.late, waiting = {}, []
        for k in self.steps:
            self.late[k] = waiting
            waiting = [r for op, r in self.lag[k] if op == "W"]
        self.last = waiting + [r for op, r in self.tail if op == "W"] if drain else []
        self.behind = 3 if self.m else None
        a, m = self.a, self.m
        self.first = {0: [("XT", "A")] * a, 3: [("XT", "M")] * m, 5: [("XT", "C")] * m}
        early = {1: ("Q", "A", 0), 2: ("V", "A", 0), 4: ("DOWN", 1), 6: ("Q", "C", 0), 7: ("V", "C", 0)}
        mid = {0: [("K", "A", 0)], 3: [("UP", 0), ("UP", 1)], 5: [("K", "C", 0)]}
        fill = {0: [("K", "A", 1)], 1: [("Q", "A", 1)], 2: [("V", "A", 1)],
                3: [("UP", j) for j in range(2, FC)] + [("DOWN", 0)],
                5: [("K", "C", 1)], 6: [("Q", "C", 1)], 7: [("V", "C", 1)]}
        present = [k for k in range(STEPS) if (a if k < 3 else m)]
        self.early = {k: [early[k]] for k in present if k in early}
        self.mid = {k: mid[k] for k in present if k in mid}
        self.fill = {k: fill[k] for k in present if k in fill}
        if before is None:
            for k, n in BIAS_STEPS.items():
                self.fill[k] = self.fill.get(k, []) + [("BIAS", n)]
        self.use, self.high = {}, {}
        for k in range(STEPS):
            lag = self.lag.get(k, [])
            self.number(self.first.get(k, []) + only("V", lag) + self.early.get(k, [])
                        + self.mid.get(k, []) + only("W", lag) + self.fill.get(k, []))
            if k == self.steps[-1]:
                self.number(self.tail)
        if before is None:
            self.unit0 = self.use0 = self.high0 = 0
        else:
            self.unit0 = before.unit0 + before.turns * len(before.order)
            self.use0 = before.use0 + before.turns * len(before.use)
            self.high0 = before.high0 + before.turns * len(before.high)
        assert not self.looped or len(self.use) % BANKS == 0

    def number(self, ops):
        for use in [use for op in ops for use in bank_uses(op)]:
            self.use[use] = len(self.use)
            if use[0] in ("XT", "Q", "K", "O"):
                self.high[use] = len(self.high)


def only(kind, ops):
    return [op for op in ops if op[0] == kind]


def bank_uses(op):
    if op[0] == "T":
        return []
    if op[0] == "XT":
        return [op + (c,) for c in range(KC)]
    return [("O", op[1])] if op[0] == "V" and len(op) == 2 else [op]


def make_shapes():
    shapes, before = [], None
    for it, stages, following in [(0, "A", True), (1, "AM", True), ("loop", "AMC", True),
                                  (NG - 1, "AMC", False), (NG, "MC", False), (NG + 1, "C", False)]:
        before = Shape(it, stages, following, before, it in (0, NG, NG + 1))
        shapes.append(before)
    return shapes


class Turn:

    def __init__(self, shape, it):
        self.s, self.it = shape, it
        self.group_a, self.group_m, self.group_c = it, it - 1, it - 2

    def grown(self, base, each):
        return self.it * each + (base - 2 * each) if self.s.looped else base

    def unit(self, r):
        order = self.s.order if r >= 0 else self.s.before.order
        stage, b = order[r]
        return self.grown(self.s.unit0 + r, len(self.s.order)), stage, b

    def group(self, r):
        _, stage, _ = self.unit(r)
        return (self.group_a if stage == "A" else self.group_c) - (1 if r < 0 else 0)

    def bank(self, key, earlier=False):
        s = self.s
        n = s.use0 + (s.before.use[key] - len(s.before.use) if earlier else s.use[key])
        return n % BANKS, self.grown(n // BANKS + 1, len(s.use) // BANKS)

    def high(self, key):
        return self.grown(self.s.high0 + self.s.high[key] + 1, len(self.s.high))


def run_pipeline(eng, shapes, body):
    for s in shapes:
        if s.looped:
            with eng.Fori(2, NG - 1) as it:
                body(Turn(s, it))
        else:
            body(Turn(s, s.it))


def wait(eng, sem, count):
    if not (isinstance(count, int) and count <= 0):
        eng.wait_ge(sem, count)


def build(nc, T, out):
    ctx = ExitStack()
    with ctx:
        def sb(name, shape, dt=F32):
            return ctx.enter_context(nc.sbuf_tensor(name, shape, dt))

        def sem(name):
            return ctx.enter_context(nc.semaphore(name))

        weight = {}
        for name in ("q0", "k0", "v0", "o0", "q1", "k1", "v1", "o1"):
            weight[name] = sb("w_" + name, [P, 2, KC, D], F32R)
        w_up = sb("w_up", [P, 2, KC, FF], F32R)
        w_down = sb("w_down", [P, 2, FC, D], F32R)
        row_bias = sb("row_bias", [P, len("AMC"), D])
        ident = sb("ident", [P, P])
        gamma, beta = sb("gamma", [P, D]), sb("beta", [P, D])
        cols = sb("cols", [P, 28])
        ready_cols = sb("ready_cols", [P, 16])
        half, fence, table_turn = sb("half", [P, GB]), sb("fence", [P, 16]), sb("table_turn", [P, 1])

        normed = sb("normed", [P, 2, KC, TOK], F32R)
        queries = {"A": sb("queries_a", [P, 2, KC, TOK], F32R), "C": sb("queries_c", [P, 2, KC, TOK], F32R)}
        key_blocks = sb("key_blocks", [P, KC, 2, HC, TOK], F32R)
        values = {"A": sb("values_a", [P, GB, D]), "C": sb("values_c", [P, GB, D])}
        scores = sb("scores", [P, 2, H, P])
        negmax, total, inverse = sb("negmax", [P, 2, H]), sb("total", [P, 2, H]), sb("inverse", [P, 2, H])
        probs_t = sb("probs_t", [P, H, P])
        heads_t = sb("heads_t", [P, 2, KC, P], F32R)
        hidden_raw = sb("hidden_raw", [P, 2, TOK])
        hidden = sb("hidden", [P, FC, 2, TOK], F32R)
        keys = hidden[:, FC - KC:FC, :, :]
        x_in = sb("x_in", [P, GB, D])
        res_a = sb("res_a", [P, GB, D])
        x_two = sb("x_two", [P, GB, D])
        res_c = sb("res_c", [P, GB, D])
        adj = {"A": sb("adj_a", [P, GB, P]), "C": sb("adj_c", [P, GB, P])}
        adj_tmp = sb("adj_tmp", [P, GB, P])
        stats = {n: sb("stats_" + n, [P, GB, 6]) for n in "AMC"}
        moments = {n: sb("moments_" + n, [P, GB, 2]) for n in "AMC"}
        spread = {n: sb("spread_" + n, [P, GB]) for n in "AMC"}
        rstd = {n: sb("rstd_" + n, [P, GB]) for n in "AMC"}

        p_scores = ctx.enter_context(nc.psum_tensor("p_scores", [P, KC, HC * P], F32))
        p_probs = ctx.enter_context(nc.psum_tensor("p_probs", [P, KC, HC * P], F32))
        p_bank = [ctx.enter_context(nc.psum_tensor(f"p_bank{i}", [P, TOK], F32)) for i in range(BANKS)]

        piece_loaded = [sem(f"piece{n}_loaded") for n in range(8)]
        cols_loaded, more_cols_loaded = sem("cols_loaded"), sem("more_cols_loaded")
        piece_scaled, piece_high, piece_done = sem("piece_scaled"), sem("piece_high"), sem("piece_done")
        bias_products, setup_vector, zeroed = sem("bias_products"), sem("setup_vector"), sem("zeroed")
        x_loaded, res_a_loaded, res_c_loaded = sem("x_loaded"), sem("res_a_loaded"), sem("res_c_loaded")
        adj_loaded = {"A": sem("adj_a_loaded"), "C": sem("adj_c_loaded")}
        blocks_loaded = {n: [sem(f"blocks_{n.lower()}_loaded{i}") for i in range(2)] for n in "AC"}
        stored = sem("stored")
        filled = [sem(f"filled{i}") for i in range(BANKS)]
        scores_made, probs_turned = sem("scores_made"), sem("probs_turned")
        drained = [sem(f"drained{i}") for i in range(BANKS)]
        high_made, exps_made, turned_out0 = sem("high_made"), sem("exps_made"), sem("turned_out0")
        masked_made, inverses_made, turned_out1 = sem("masked_made"), sem("inverses_made"), sem("turned_out1")
        hidden_high, hidden_made = sem("hidden_high"), sem("hidden_made")
        ln_steps = {n: sem("ln_steps_" + n) for n in "AMC"}
        ln_applied = {n: sem("ln_applied_" + n) for n in "AMC"}
        mask_steps = {"A": sem("mask_steps_a"), "C": sem("mask_steps_c")}
        biased = {n: sem("biased_" + n.lower()) for n in "AMC"}
        probs_made, gained, finished = sem("probs_made"), sem("gained"), sem("finished")
        rstd_made = {n: sem("rstd_made_" + n) for n in "AMC"}

        x_view = T["x"].rearrange("b s d -> s b d")
        out_view = out.rearrange("b s d -> s b d")
        adj_view = T["adj"].rearrange("b q k -> q b k")

        def w_view(name):
            return T[name].rearrange("(c p) n -> p c n", p=P)

        L0, L1 = "L0_gnn_", "L1_gnn_"
        vectors = [(L0 + "ln1_g", KC), (L0 + "ln2_g", KC), (L0 + "ln1_b", KC), (L0 + "ln2_b", KC),
                   (L0 + "bq", KC), (L0 + "bk", KC), (L0 + "bv", KC), (L0 + "b1", FC),
                   (L1 + "bq", KC), (L1 + "bk", KC), (L1 + "bv", KC)]
        at, col = {}, 0
        for name, n in vectors:
            at[name] = col
            col += n
        assert col == cols.shape[1]
        rows = [("o0", L0 + "bo"), ("down", L0 + "b2"), ("o1", L1 + "bo")]
        QSCALE = -1.0 / float(np.sqrt(HD))

        W = KC * D
        flat = lambda t: t.rearrange("p c n -> p (c n)")
        whole = lambda name: (lambda part: flat(weight[name][:, part]))
        as_piece = lambda x: x.rearrange("p a b -> p (a b)")
        later = [as_piece(x[:, :, :]) for x in (res_c, values["C"], hidden_raw, probs_t)]
        staged = [as_piece(scores[:, 0]), as_piece(scores[:, 1])] + later + later[:2]
        scaled = as_piece(x_two[:, :, :])
        w1, w2 = w_view(L0 + "w1"), w_view(L0 + "w2")
        g1 = [cols[:, at[L0 + "ln1_g"] + c:at[L0 + "ln1_g"] + c + 1] for c in range(KC)]
        g2 = [cols[:, at[L0 + "ln2_g"] + c:at[L0 + "ln2_g"] + c + 1] for c in range(KC)]
        pieces = [
            ([w_view(L0 + "wq"), w_view(L0 + "wk")], [whole("q0"), whole("k0")],
             [(0, D, g1[0], QSCALE), (D, D, g1[1], QSCALE), (2 * D, D, g1[0], 1.0), (3 * D, D, g1[1], 1.0)]),
            ([w_view(L0 + "wv"), w_view(L0 + "wo")], [whole("v0"), whole("o0")],
             [(0, D, g1[0], 1.0), (D, D, g1[1], 1.0), (2 * D, 2 * D, 1.0, 1.0)]),
            ([w1[:, 0:1]], [lambda part: w_up[:, part, 0]], [(0, FF, g2[0], 1.0)]),
            ([w1[:, 1:2]], [lambda part: w_up[:, part, 1]], [(0, FF, g2[1], 1.0)]),
            ([w2[:, 0:4]], [lambda part: flat(w_down[:, part, 0:4])], [(0, FF, 1.0, 1.0)]),
            ([w2[:, 4:8]], [lambda part: flat(w_down[:, part, 4:8])], [(0, FF, 1.0, 1.0)]),
            ([w_view(L1 + "Wq"), w_view(L1 + "Wk")], [whole("q1"), whole("k1")],
             [(0, W, 1.0, QSCALE), (W, W, 1.0, 1.0)]),
            ([w_view(L1 + "Wv"), w_view(L1 + "Wo")], [whole("v1"), whole("o1")], [(0, 2 * W, 1.0, 1.0)]),
        ]
        assert len(pieces) == len(staged) == len(piece_loaded)
        ZEROED = 4
        EARLY_VECTOR = 7
        SETUP_VECTOR = 13
        spread_bv = adj["C"][:, :, :]
        early_vectors = ["ln1_g", "ln1_b", "bq", "bk", "bv"]
        EARLY_COLS = 16 * (len(early_vectors) + 1)
        MORE_COLS = 16 * (len(vectors) + len(rows) + 2) - EARLY_COLS

        def start(eng):
            eng.wait_ge(piece_done, EARLY_PIECES)
            eng.wait_ge(setup_vector, EARLY_VECTOR)
            eng.wait_ge(zeroed, ZEROED)

        def setup_over(eng, t):
            if t.s.before is not None and t.s.before.before is None:
                eng.wait_ge(piece_done, len(pieces))
                eng.wait_ge(setup_vector, SETUP_VECTOR)
                for n in BIAS_STEPS.values():
                    bank, number = t.bank(("BIAS", n), earlier=True)
                    eng.wait_ge(drained[bank], number)

        def copied(eng, t, before):
            stage = {"A": "C" if t.s.c else "A", "C": "A" if t.s.a else "C", "M": "A" if t.s.a else "C"}[before]
            group = t.group_c + 1 if stage == "C" else t.group_a if before == "A" else t.group_a + 1
            for blocks in blocks_loaded[stage]:
                wait(eng, blocks, group * HC * 16)

        def split_part(kind, stage, part, c):
            return queries[stage][:, part, c, :] if kind == "Q" else keys[:, c, part, :]

        shapes = make_shapes()
        weights_of = {"A": ("q0", "k0", "v0", "o0"), "C": ("q1", "k1", "v1", "o1")}
        residual = {"A": res_a, "C": res_c}
        block = ctx.enter_context(nc.Block())

        @block.sync
        def _(sp):
            def load_vectors(names, loaded):
                for name, n in vectors:
                    if name in names:
                        sp.dma_start(cols[:, at[name]:at[name] + n], T[name].rearrange("(c p) -> p c", p=P),
                                     allow_slow_non_contiguous=True).then_inc(loaded, 16)

            def load_row(i, loaded):
                sp.dma_start(row_bias[:, i, :], T[rows[i][1]].partition_broadcast(P)).then_inc(loaded, 16)

            def load_piece(n):
                loads = pieces[n][0]
                for i, src in enumerate(loads):
                    width = 2 * W // len(loads)
                    dst = staged[n][:, i * width:(i + 1) * width].rearrange("p (c n) -> p c n", n=src.shape[2])
                    sp.dma_start(dst, src).then_inc(piece_loaded[n], 16)

            early = [L0 + name for name in early_vectors]
            load_vectors(early[:2], cols_loaded)
            load_piece(0)
            load_vectors(early[2:], cols_loaded)
            load_row(0, cols_loaded)
            sp.dma_start(x_in[:, :, :], x_view[:, 0:GB, :]).then_inc(x_loaded, 16)
            load_piece(1)
            sp.dma_start(adj["A"][:, :, :].bitcast(I32), adj_view[:, 0:GB, :]).then_inc(adj_loaded["A"], 16)
            load_vectors([name for name, _ in vectors if name not in early], more_cols_loaded)
            for i in range(1, len(rows)):
                load_row(i, more_cols_loaded)
            sp.dma_start(gamma[:, :], T[L1 + "gamma"].partition_broadcast(P)).then_inc(more_cols_loaded, 16)
            sp.dma_start(beta[:, :], T[L1 + "beta"].partition_broadcast(P)).then_inc(more_cols_loaded, 16)
            for n in range(EARLY_PIECES, EARLY_PIECES + len(later)):
                load_piece(n)
            start(sp)

            def drained_use(t, use):
                bank, number = t.bank(use)
                return drained[bank], number

            def load_blocks(stage, half, condition):
                sp.wait_ge(*condition)
                two = slice(half * TOK // 2, (half + 1) * TOK // 2)
                for j in range(HC):
                    rows_j = slice(HD * j, HD * (j + 1))
                    sp.dma_start(key_blocks[rows_j, :, :, j, two].bitcast(F32), keys[rows_j, :, :, two].bitcast(F32)
                                 ).then_inc(blocks_loaded[stage][half], 16)

            def store(t, b):
                sp.wait_ge(finished, t.group_c * GB + b + 1)
                sp.dma_start(out_view[:, bass.ds(t.group_c * GB + b, 1), :], res_c[:, b:b + 1, :]).then_inc(stored, 16)

            def body(t):
                s = t.s
                setup_over(sp, t)
                unit0 = t.grown(s.unit0, len(s.order))
                if s.before is None:
                    load_blocks("A", 0, drained_use(t, ("K", "A", 1)))
                    load_blocks("A", 1, drained_use(t, ("K", "A", 1)))
                if s.a and s.following:
                    sp.wait_ge(*drained_use(t, ("XT", "A", 1)))
                    sp.dma_start(x_in[:, :, :], x_view[:, bass.ds((t.group_a + 1) * GB, GB), :]).then_inc(x_loaded, 16)
                if s.before is None:
                    for n in range(EARLY_PIECES + len(later), len(pieces)):
                        sp.wait_ge(piece_scaled, n - len(later) + 1)
                        sp.wait_ge(*drained_use(t, ("BIAS", n - len(later))))
                        load_piece(n)
                if s.a and s.before is not None:
                    last_use = (masked_made, (unit0 + 2) * H) if s.c else drained_use(t, ("K", "A", 1))
                    load_blocks("A", 0, last_use)
                    load_blocks("A", 1, (masked_made, (unit0 + GB) * H) if s.c else last_use)
                if s.m:
                    if s.c:
                        sp.wait_ge(masked_made, (unit0 + GB) * H)
                    sp.dma_start(adj["C"][:, :, :].bitcast(I32), adj_view[:, bass.ds(t.group_m * GB, GB), :]
                                 ).then_inc(adj_loaded["C"], 16)
                if s.c:
                    store(t, 0)
                    store(t, 1)
                if s.a:
                    if s.m:
                        sp.wait_ge(*drained_use(t, ("DOWN", 1)))
                    sp.dma_start(res_a[:, :, :], x_view[:, bass.ds(t.group_a * GB, GB), :]).then_inc(res_a_loaded, 16)
                if s.c:
                    store(t, 2)
                if s.m:
                    load_blocks("C", 0, drained_use(t, ("K", "C", 1)))
                if s.c:
                    store(t, 3)
                if s.m:
                    load_blocks("C", 1, (masked_made, (unit0 + len(s.order)) * H) if s.a
                                else drained_use(t, ("K", "C", 1)))
                    if s.c:
                        sp.wait_ge(stored, (t.group_c + 1) * GB * 16)
                    if not (s.a and s.c):
                        sp.wait_ge(*drained_use(t, ("DOWN", 1)))
                    sp.dma_start(res_c[:, :, :], x_two[:, :, :]).then_inc(res_c_loaded, 16)
                if s.a and s.following:
                    sp.wait_ge(masked_made, (unit0 + len(s.order)) * H)
                    sp.dma_start(adj["A"][:, :, :].bitcast(I32), adj_view[:, bass.ds((t.group_a + 1) * GB, GB), :]
                                 ).then_inc(adj_loaded["A"], 16)

            run_pipeline(sp, shapes, body)
            sp.wait_ge(stored, NG * GB * 16)

        @block.gpsimd
        def _(pool):
            nc.gpsimd.memset(ident[:, :], 0.0).then_inc(zeroed, 1)
            nc.gpsimd.memset(half[:, :], -0.5).then_inc(zeroed, 1)
            nc.gpsimd.memset(key_blocks[:, :, :, :, :].bitcast(F32), 0.0).then_inc(zeroed, 1)
            pool.wait_ge(zeroed, 3)
            nc.gpsimd.affine_select(out=ident[:, :], in_=ident[:, :], compare_op=ALU.not_equal, fill=1.0,
                                    base=0, pattern=[[-1, P]], channel_multiplier=1).then_inc(zeroed, 1)
            def make_rstd(n, b0, b1, steps):
                pool.wait_ge(ln_steps[n], steps)
                nc.gpsimd.tensor_tensor(rstd[n][:, b0:b1], spread[n][:, b0:b1], half[:, b0:b1], ALU.pow
                                        ).then_inc(rstd_made[n], 1)

            make_rstd("A", 0, GB, 3)
            start(pool)

            def rstd_of(t, ops):
                for op, r in ops:
                    if op == "W":
                        _, stage, b = t.unit(r)
                        if stage == "A" and b == GB - 1:
                            make_rstd("M", 0, GB, t.group(r) * 3 + 3)
                        if stage == "C":
                            make_rstd("C", b, b + 1, (t.group(r) * GB + b) * 3 + 3)

            def add_bias(stage, sem, count):
                pool.wait_ge(sem, count)
                x = res_c if stage == "C" else res_a
                for b in range(0, GB, 2):
                    row = row_bias[:, "AMC".index(stage):"AMC".index(stage) + 1, :].broadcast_to([P, 2, D])
                    nc.gpsimd.tensor_tensor(x[:, b:b + 2, :], x[:, b:b + 2, :], row, ALU.add
                                            ).then_inc(biased[stage], 1)

            def finish(t, r):
                _, stage, b = t.unit(r)
                if stage == "C":
                    unit = t.group(r) * GB + b
                    pool.wait_ge(ln_applied["C"], unit + 1)
                    nc.gpsimd.tensor_tensor(res_c[:, b], res_c[:, b], gamma[:, :], ALU.mult).then_inc(gained, 1)
                    pool.wait_ge(gained, unit + 1)
                    nc.gpsimd.tensor_tensor(res_c[:, b], res_c[:, b], beta[:, :], ALU.add).then_inc(finished, 1)

            def body(t):
                s = t.s
                setup_over(pool, t)
                for k in range(STEPS):
                    def make_probs(c):
                        u, _, _ = t.unit(s.steps.index(k))
                        pool.wait_ge(inverses_made, u * KC + c + 1)
                        heads = slice(HC * c, HC * (c + 1))
                        rows_c = scores[:, k % 2, heads, :]
                        nc.gpsimd.tensor_tensor(
                            rows_c, rows_c, inverse[:, k % 2, heads].unsqueeze(2).broadcast_to([P, HC, P]),
                            ALU.mult).then_inc(probs_made, 1)

                    for c in range(KC) if k in s.units and k != s.behind else []:
                        make_probs(c)
                    for r in s.late.get(k, []):
                        finish(t, r)
                    rstd_of(t, s.lag.get(k, []))
                    if k == 1 and s.c:
                        add_bias("C", res_c_loaded, (t.group_c + 1) * 16)
                    if k == 3 and s.m:
                        add_bias("M", ln_applied["M"], t.group_m + 1)
                    if k == 5 and s.before is None:
                        bank, number = t.bank(("BIAS", 1))
                        pool.wait_ge(drained[bank], number)
                    if k == 5 and s.a:
                        add_bias("A", res_a_loaded, (t.group_a + 1) * 16)
                    if k == 3 and s.following:
                        make_rstd("A", 0, GB, (t.group_a + 1) * 3 + 3)
                    for c in range(KC) if k in s.units and k == s.behind else []:
                        make_probs(c)
                    if k == s.steps[-1]:
                        rstd_of(t, s.tail)
                        for r in s.last:
                            finish(t, r)

            run_pipeline(pool, shapes, body)

        @block.scalar
        def _(act):
            def split_high(n):
                targets = pieces[n][1]
                act.wait_ge(piece_scaled, n + 1)
                width = 2 * W // len(targets)
                for i, target in enumerate(targets):
                    last = nc.scalar.activation(target(HI), scaled[:, i * width:(i + 1) * width], ACT.Copy)
                last.then_inc(piece_high, 1)

            for n in range(EARLY_PIECES):
                split_high(n)
            start(act)

            def exps(t, k, c):
                u, _, _ = t.unit(t.s.steps.index(k))
                for h in range(HC * c, HC * (c + 1)):
                    if h % 2 == 0:
                        act.wait_ge(masked_made, u * H + h + 2)
                    last = nc.scalar.activation(scores[:, k % 2, h], scores[:, k % 2, h], ACT.Exp, scale=-1.0,
                                                bias=negmax[:, k % 2, h:h + 1], accum_out=total[:, k % 2, h:h + 1])
                last.then_inc(exps_made, 1)

            def evacuate(t, op):
                kind, what = op[0], op[1]
                for use in bank_uses(op):
                    bank, number = t.bank(use)
                    src = p_bank[bank]
                    act.wait_ge(filled[bank], number)
                    if kind == "XT":
                        nc.scalar.activation(normed[:, HI, use[2], :], src[:, :], ACT.Copy).then_inc(high_made, 1)
                    elif kind in "QK":
                        if kind == "K":
                            copied(act, t, what)
                        bias = 4 * (what == "C") + 2 * (kind == "K") + use[2]
                        nc.scalar.activation(split_part(kind, what, HI, use[2]), src[:, :], ACT.Identity,
                                             bias=ready_cols[:, bias:bias + 1]).then_inc(high_made, 1)
                    elif kind == "V":
                        dst = values[what][:, 2 * use[2]:2 * use[2] + 2, :].rearrange("p g n -> p (g n)")
                        nc.scalar.activation(dst, src[:, :], ACT.Copy).then_inc(drained[bank], 1)
                    elif kind == "UP":
                        j = use[1]
                        wait(act, hidden_made, t.group_m * FC + j - 1)
                        nc.scalar.activation(hidden_raw[:, j % 2], src[:, :], ACT.Gelu,
                                             bias=ready_cols[:, 8 + j:9 + j]).then_inc(drained[bank], 1)

            def turned(t, r):
                u, _, _ = t.unit(r)
                act.wait_ge(probs_turned, u * KC + 1)
                nc.scalar.activation(probs_t[:, 0:HC].rearrange("p h n -> p (h n)"), p_probs[:, 0, :], ACT.Copy
                                     ).then_inc(turned_out0, 1)

            def heads_high(t, r):
                bank, number = t.bank(("O", r))
                act.wait_ge(filled[bank], number)
                nc.scalar.activation(heads_t[:, HI].rearrange("p c n -> p (c n)"), p_bank[bank][:, 0:KC * P],
                                     ACT.Copy).then_inc(high_made, 1)

            def body(t):
                s = t.s
                setup_over(act, t)
                for k in range(STEPS):
                    lag = s.lag.get(k, [])
                    for op in s.first.get(k, []):
                        evacuate(t, op)
                    for _, r in only("V", lag):
                        heads_high(t, r)
                    if k in s.units and k != s.behind:
                        exps(t, k, 0)
                    for op in s.early.get(k, []):
                        if op[0] != "DOWN":
                            evacuate(t, op)
                    if k in s.units and k != s.behind:
                        exps(t, k, 1)
                    for _, r in only("T", lag):
                        turned(t, r)
                    for op in s.mid.get(k, []) + s.fill.get(k, []):
                        if op[0] not in ("DOWN", "BIAS"):
                            evacuate(t, op)
                    for n in PIECE_STEPS.get(k, []) if s.before is None else []:
                        split_high(n)
                    if k == s.behind and k in s.units:
                        exps(t, k, 0)
                        exps(t, k, 1)
                    elif k == s.behind:
                        nc.scalar.activation(table_turn[:, :], half[:, 0:1], ACT.Exp)
                    for op, r in s.tail if k == s.steps[-1] else []:
                        if op == "T":
                            turned(t, r)
                        if op == "V":
                            heads_high(t, r)

            run_pipeline(act, shapes, body)

        @block.vector
        def _(dve):
            step, taken = [0], [0]

            def then(instruction):
                step[0] += 1
                instruction.then_inc(setup_vector, 1)
                dve.wait_ge(setup_vector, step[0])

            def take_wait():
                at_col = taken[0] % fence.shape[1]
                taken[0] += 1
                nc.vector.memset(fence[:, at_col:at_col + 1], 0.0)

            def layer_norm_steps(n, src, b0, b1, done, measure):
                if measure:
                    for b in range(b0, b1):
                        last = nc.vector.bn_stats(stats[n][:, b, :], src[:, b, :])
                    last.then_inc(ln_steps[n], 1)
                dve.wait_ge(ln_steps[n], done + 1)
                take_wait()
                for b in range(b0, b1):
                    last = nc.vector.bn_aggr(moments[n][:, b, :], stats[n][:, b, :])
                last.then_inc(ln_steps[n], 1)
                dve.wait_ge(ln_steps[n], done + 2)
                nc.vector.tensor_scalar(spread[n][:, b0:b1], moments[n][:, b0:b1, 1], EPS, None, ALU.add
                                        ).then_inc(ln_steps[n], 1)

            def normalize(n, src, dst, b0, b1, made):
                dve.wait_ge(rstd_made[n], made)
                for b in range(b0, b1):
                    last = nc.vector.tensor_scalar(dst[:, b, :], src[:, b, :], moments[n][:, b, 0:1],
                                                   rstd[n][:, b:b + 1], ALU.subtract, ALU.mult)
                last.then_inc(ln_applied[n], 1)

            def mask_a(group):
                a = adj["A"][:, :, :]
                dve.wait_ge(adj_loaded["A"], (group + 1) * 16)
                nc.vector.scalar_tensor_tensor(out=adj_tmp[:, :, :], in0=a.bitcast(I32), scalar=-0.1,
                                               in1=a.bitcast(I32), op0=ALU.mult, op1=ALU.mult
                                               ).then_inc(mask_steps["A"], 1)
                dve.wait_ge(mask_steps["A"], group * 3 + 1)
                nc.vector.tensor_scalar(a, a.bitcast(I32), 0.0, MASKED, ALU.is_le, ALU.mult
                                        ).then_inc(mask_steps["A"], 1)
                dve.wait_ge(mask_steps["A"], group * 3 + 2)
                nc.vector.tensor_tensor(a, a, adj_tmp[:, :, :], ALU.add).then_inc(mask_steps["A"], 1)
                dve.wait_ge(mask_steps["A"], group * 3 + 3)

            def mask_c(group):
                a = adj["C"][:, :, :]
                dve.wait_ge(adj_loaded["C"], (group + 1) * 16)
                nc.vector.tensor_scalar(a, a.bitcast(I32), 0.0, MASKED, ALU.is_equal, ALU.mult
                                        ).then_inc(mask_steps["C"], 1)
                dve.wait_ge(mask_steps["C"], group + 1)

            def split_piece(n):
                _, targets, factors = pieces[n]
                dve.wait_ge(piece_loaded[n], 16 * len(pieces[n][0]))
                if n:
                    dve.wait_ge(piece_high, n)
                    dve.wait_ge(piece_done, n)
                for first, width, gain, factor in factors:
                    last = nc.vector.tensor_scalar(scaled[:, first:first + width], staged[n][:, first:first + width],
                                                   gain, factor, ALU.mult, ALU.mult)
                last.then_inc(piece_scaled, 1)
                dve.wait_ge(piece_high, n + 1)
                width = 2 * W // len(targets)
                for i, target in enumerate(targets):
                    last = nc.vector.tensor_tensor(target(LO), scaled[:, i * width:(i + 1) * width],
                                                   target(HI).bitcast(F32), ALU.subtract)
                last.then_inc(piece_done, 1)

            biases = cols[:, at[L0 + "bq"]:at[L0 + "bq"] + 3 * KC]
            up_bias = cols[:, at[L0 + "b1"]:at[L0 + "b1"] + FC]

            def later_biases():
                dve.wait_ge(more_cols_loaded, MORE_COLS)
                for c in range(KC):
                    q, bk, bv = at[L1 + "bq"] + c, at[L1 + "bk"] + c, at[L1 + "bv"] + c
                    then(nc.vector.tensor_scalar(ready_cols[:, 4 + c:5 + c], cols[:, q:q + 1], QSCALE, None, ALU.mult))
                    then(nc.vector.tensor_copy(ready_cols[:, 6 + c:7 + c], cols[:, bk:bk + 1]))
                    then(nc.vector.tensor_scalar(spread_bv[:, KC + c, :], spread_bv[:, KC + c, :], cols[:, bv:bv + 1],
                                                 None, ALU.mult))

            dve.wait_ge(cols_loaded, EARLY_COLS)
            then(nc.vector.memset(spread_bv, 1.0))
            split_piece(0)
            dve.wait_ge(x_loaded, 16)
            layer_norm_steps("A", x_in, 0, GB, 0, True)
            split_piece(1)
            normalize("A", x_in, x_in, 0, GB, 1)
            dve.wait_ge(bias_products, EARLY_PIECES)
            sums = p_bank[0][:, 0:3 * KC * KC].rearrange("p (x c) -> p c x", c=KC)
            then(nc.vector.tensor_tensor(biases, sums[:, 0], biases, ALU.add))
            then(nc.vector.tensor_tensor(biases, sums[:, 1], biases, ALU.add))
            nc.vector.tensor_scalar(ready_cols[:, 0:2], biases[:, 0:2], QSCALE, None, ALU.mult)
            then(nc.vector.tensor_copy(ready_cols[:, 2:4], biases[:, 2:4]))
            for c in range(KC):
                then(nc.vector.tensor_scalar(spread_bv[:, c, :], spread_bv[:, c, :], biases[:, 4 + c:5 + c],
                                             None, ALU.mult))
            assert step[0] == EARLY_VECTOR - 1, step[0]
            mask_a(0)
            then(nc.vector.memset(fence[:, :], 0.0))
            start(dve)

            def mask_scores(t, k, c):
                u, stage, b = t.unit(t.s.steps.index(k))
                dve.wait_ge(scores_made, u * KC + c + 1)
                take_wait()
                for h in range(HC * c, HC * (c + 1)):
                    nc.vector.tensor_tensor_reduce(
                        out=scores[:, k % 2, h], in0=p_scores[:, c, (h % HC) * P:(h % HC + 1) * P],
                        in1=adj[stage][:, b, :], scale=1.0, scalar=LARGEST, op0=ALU.add, op1=ALU.min,
                        accum_out=negmax[:, k % 2, h:h + 1]).then_inc(masked_made, 1)

            def invert(t, k, c):
                u, _, _ = t.unit(t.s.steps.index(k))
                dve.wait_ge(exps_made, u * KC + c + 1)
                heads = slice(HC * c, HC * (c + 1))
                nc.vector.reciprocal(inverse[:, k % 2, heads], total[:, k % 2, heads]).then_inc(inverses_made, 1)

            def evacuate(t, op):
                kind, what = op[0], op[1]
                for use in bank_uses(op):
                    bank, number = t.bank(use)
                    src = p_bank[bank]
                    if kind == "XT":
                        dve.wait_ge(high_made, t.high(use))
                        hi, lo = normed[:, HI, use[2], :], normed[:, LO, use[2], :]
                        nc.vector.tensor_tensor(lo, src[:, :], hi.bitcast(F32), ALU.subtract).then_inc(drained[bank], 1)
                    elif kind in "QK":
                        dve.wait_ge(high_made, t.high(use))
                        bias = 4 * (what == "C") + 2 * (kind == "K") + use[2]
                        nc.vector.scalar_tensor_tensor(
                            out=split_part(kind, what, LO, use[2]), in0=src[:, :], scalar=ready_cols[:, bias:bias + 1],
                            in1=split_part(kind, what, HI, use[2]).bitcast(F32), op0=ALU.add, op1=ALU.subtract
                        ).then_inc(drained[bank], 1)
                    elif kind == "BIAS":
                        dve.wait_ge(filled[bank], number)
                        n = use[1]
                        if n in (1, len(pieces) - 1):
                            row = row_bias[:, 0 if n == 1 else 2, :]
                            add = (row, src[:, 0:D], row)
                        elif n == 2:
                            add = (up_bias, src[:, 0:FC], up_bias)
                        else:
                            bank2, number2 = t.bank(("BIAS", 2))
                            dve.wait_ge(drained[bank2], number2)
                            add = (ready_cols[:, 8:16], src[:, 0:FC], up_bias)
                        nc.vector.tensor_tensor(*add, ALU.add).then_inc(drained[bank], 1)
                    elif kind == "UP":
                        j = use[1]
                        if j == FC - KC:
                            copied(dve, t, "M")
                        dve.wait_ge(drained[bank], number)
                        nc.vector.tensor_copy(hidden[:, j, HI, :], hidden_raw[:, j % 2]).then_inc(hidden_high, 1)
                        dve.wait_ge(hidden_high, t.group_m * FC + j + 1)
                        nc.vector.tensor_tensor(hidden[:, j, LO, :], hidden_raw[:, j % 2],
                                                hidden[:, j, HI, :].bitcast(F32), ALU.subtract
                                                ).then_inc(hidden_made, 1)
                    elif kind == "DOWN":
                        dve.wait_ge(filled[bank], number)
                        dve.wait_ge(biased["M"], t.group_m * 2 + what + 1)
                        two = slice(2 * what, 2 * what + 2)
                        both = lambda x: x[:, two, :].rearrange("p g n -> p (g n)")
                        nc.vector.tensor_tensor(both(x_two), src[:, :], both(res_a), ALU.add
                                                ).then_inc(drained[bank], 1)

            def turned(t, r):
                u, _, _ = t.unit(r)
                dve.wait_ge(probs_turned, u * KC + 2)
                nc.vector.tensor_copy(probs_t[:, HC:H].rearrange("p h n -> p (h n)"), p_probs[:, 1, :]
                                      ).then_inc(turned_out1, 1)

            def heads_low(t, r):
                bank, _ = t.bank(("O", r))
                dve.wait_ge(high_made, t.high(("O", r)))
                part = lambda i: heads_t[:, i].rearrange("p c n -> p (c n)")
                nc.vector.tensor_tensor(part(LO), p_bank[bank][:, 0:KC * P], part(HI).bitcast(F32), ALU.subtract
                                        ).then_inc(drained[bank], 1)

            def add_residual(t, r):
                _, stage, b = t.unit(r)
                group = t.group(r)
                bank, number = t.bank(("W", r))
                dve.wait_ge(filled[bank], number)
                dve.wait_ge(biased[stage], group * 2 + b // 2 + 1)
                x = residual[stage]
                nc.vector.tensor_tensor(x[:, b, :], p_bank[bank][:, 0:D], x[:, b, :], ALU.add
                                        ).then_inc(drained[bank], 1)
                dve.wait_ge(drained[bank], number)
                if stage == "C":
                    layer_norm_steps("C", x, b, b + 1, (group * GB + b) * 3, True)
                else:
                    last = nc.vector.bn_stats(stats["M"][:, b, :], x[:, b, :])
                    if b == GB - 1:
                        last.then_inc(ln_steps["M"], 1)
                        layer_norm_steps("M", x, 0, GB, group * 3, False)

            def apply_norm(t, r):
                _, stage, b = t.unit(r)
                group = t.group(r)
                if stage == "C":
                    normalize("C", res_c, res_c, b, b + 1, group * GB + b + 1)
                elif b == GB - 1:
                    wait(dve, res_c_loaded, group * 16)
                    normalize("M", res_a, x_two, 0, GB, group + 1)

            def prepare(t, k):
                s = t.s
                if k == 3 and s.a and s.before is not None:
                    mask_a(t.group_a)
                if k == 3 and s.following:
                    dve.wait_ge(x_loaded, (t.group_a + 2) * 16)
                    layer_norm_steps("A", x_in, 0, GB, (t.group_a + 1) * 3, True)
                if k == 4 and s.following:
                    normalize("A", x_in, x_in, 0, GB, t.group_a + 2)
                if k == 4 and s.m:
                    mask_c(t.group_m)

            def body(t):
                s = t.s
                setup_over(dve, t)
                for k in range(STEPS):
                    lag = s.lag.get(k, [])
                    for op in s.first.get(k, []):
                        evacuate(t, op)
                    if k in s.units and k != s.behind:
                        mask_scores(t, k, 0)
                    for _, r in only("V", lag):
                        heads_low(t, r)
                    for op in s.fill.get(k - 1, []):
                        if op[0] in ("Q", "K"):
                            evacuate(t, op)
                    if k in s.units and k == s.behind:
                        mask_scores(t, k, 0)
                    if k in s.units:
                        mask_scores(t, k, 1)
                    if k in s.units and k != s.behind:
                        invert(t, k, 0)
                    for r in s.late.get(k, []):
                        apply_norm(t, r)
                    for op in s.early.get(k, []):
                        if op[0] == "DOWN":
                            prepare(t, k)
                        evacuate(t, op)
                    for _, r in only("T", lag):
                        turned(t, r)
                    if k in s.units and k != s.behind:
                        invert(t, k, 1)
                    for op in s.mid.get(k, []):
                        evacuate(t, op)
                    for _, r in only("W", lag):
                        add_residual(t, r)
                    for op in s.fill.get(k, []):
                        if op[0] == "DOWN":
                            prepare(t, k)
                            if k in s.units:
                                invert(t, k, 0)
                                invert(t, k, 1)
                        if op[0] not in ("Q", "K"):
                            evacuate(t, op)
                    if s.before is None and k == 0:
                        later_biases()
                    for n in PIECE_STEPS.get(k, []) if s.before is None else []:
                        split_piece(n)
                    if not s.m:
                        prepare(t, k)
                    assert k or s.before is not None or step[0] == SETUP_VECTOR, step[0]
                    if k == s.steps[-1]:
                        for op, r in s.tail:
                            if op == "T":
                                turned(t, r)
                            if op == "V":
                                heads_low(t, r)
                            if op == "W":
                                add_residual(t, r)
                        for r in s.last:
                            apply_norm(t, r)

            run_pipeline(dve, shapes, body)

        @block.tensor
        def _(pe):
            pe.wait_ge(cols_loaded, EARLY_COLS)

            def shift_products(n, sources, psum, first, shift):
                for i, (w, kc) in enumerate(sources):
                    for m in range(w.shape[1] // P):
                        col = first(i, m, kc)
                        last = nc.tensor.matmul(psum[:, col:col + 1], w[:, m * P:(m + 1) * P],
                                                cols[:, shift + kc:shift + kc + 1], start=True, stop=True)
                return last

            def bias_through_output(n, spread0, psum):
                for c in range(KC):
                    last = nc.tensor.matmul(psum[:, 0:D], spread_bv[:, spread0 + c, :],
                                            staged[n][:, W + c * D:W + (c + 1) * D], start=(c == 0),
                                            stop=(c == KC - 1))
                return last

            b1, b2 = at[L0 + "ln1_b"], at[L0 + "ln2_b"]
            for n in range(EARLY_PIECES):
                pe.wait_ge(piece_loaded[n], 16 * len(pieces[n][0]))
                part = lambda i: staged[n][:, i * D:(i + 1) * D]
                count = KC * (2 if n == 0 else 1)
                shift_products(n, [(part(i), i % KC) for i in range(count)], p_bank[0],
                               lambda i, m, kc: (2 * n + i // KC) * KC * KC + m * KC + kc, b1
                               ).then_inc(bias_products, 1)
            start(pe)

            def bias_work(t, n):
                bank, dst = take(t, ("BIAS", n))
                pe.wait_ge(piece_loaded[n], 16 * len(pieces[n][0]))
                if n in (1, len(pieces) - 1):
                    if n > 1:
                        pe.wait_ge(setup_vector, SETUP_VECTOR)
                    last = bias_through_output(n, 0 if n == 1 else KC, dst)
                else:
                    pe.wait_ge(more_cols_loaded, MORE_COLS)
                    last = shift_products(n, [(staged[n], n - 2)], dst, lambda i, m, kc: m, b2)
                last.then_inc(filled[bank], 1)

            def take(t, use):
                bank, number = t.bank(use)
                wait(pe, drained[bank], number - 1)
                return bank, p_bank[bank]

            def three_passes(dst, products, chunks=None):
                n, total_n = 0, 3 * len(products)
                for f, (stationary, moving) in enumerate(products):
                    if chunks is not None:
                        pe.wait_ge(hidden_made, chunks + f + 1)
                    for i, j in ((HI, HI), (HI, LO), (LO, HI)):
                        last = nc.tensor.matmul(dst, stationary(i), moving(j), start=(n == 0), stop=(n == total_n - 1))
                        n += 1
                return last

            def work(t, op):
                kind, what = op[0], op[1]
                if kind == "XT":
                    src = x_in if what == "A" else x_two
                    if what != "C":
                        group = t.group_a if what == "A" else t.group_m
                        pe.wait_ge(ln_applied[what], group + 1)
                    for i in range(2):
                        if what == "C":
                            bank, number = t.bank(("DOWN", i))
                            pe.wait_ge(drained[bank], number)
                        for c, use in enumerate(bank_uses(op)):
                            bank, dst = take(t, use) if i == 0 else (t.bank(use)[0], p_bank[t.bank(use)[0]])
                            for b in range(2 * i, 2 * i + 2):
                                last = nc.tensor.transpose(dst[:, b * P:(b + 1) * P], src[:, b, c * P:(c + 1) * P],
                                                           ident[:, :])
                            if i == 1:
                                last.then_inc(filled[bank], 1)
                    return
                if kind == "BIAS":
                    bias_work(t, what)
                    return
                for use in bank_uses(op):
                    bank, dst = take(t, use)
                    if kind in "QK":
                        m = use[2]
                        w = weight[weights_of[what]["QK".index(kind)]]
                        wait_split(t, what)
                        last = three_passes(dst[:, :], [
                            (lambda i, kc=kc: w[:, i, kc, m * P:(m + 1) * P], lambda j, kc=kc: normed[:, j, kc, :])
                            for kc in range(KC)])
                    elif kind == "V":
                        w = weight[weights_of[what][2]]
                        for half_b in range(2):
                            b = 2 * use[2] + half_b
                            last = three_passes(dst[:, half_b * D:(half_b + 1) * D], [
                                (lambda i, kc=kc: normed[:, i, kc, b * P:(b + 1) * P], lambda j, kc=kc: w[:, j, kc, :])
                                for kc in range(KC)])
                    elif kind == "UP":
                        j0 = use[1]
                        wait_split(t, "M")
                        last = three_passes(dst[:, :], [
                            (lambda i, kc=kc: w_up[:, i, kc, j0 * P:(j0 + 1) * P], lambda j, kc=kc: normed[:, j, kc, :])
                            for kc in range(KC)])
                    elif kind == "DOWN":
                        for half_b in range(2):
                            b = 2 * what + half_b
                            products = [(lambda i, f=f: hidden[:, f, i, b * P:(b + 1) * P],
                                         lambda j, f=f: w_down[:, j, f, :]) for f in range(FC)]
                            chunks = t.group_m * FC if what == 0 and half_b == 0 else None
                            last = three_passes(dst[:, half_b * D:(half_b + 1) * D], products, chunks)
                    last.then_inc(filled[bank], 1)

            def wait_split(t, what):
                for c in range(KC):
                    bank, number = t.bank(("XT", what, c))
                    pe.wait_ge(drained[bank], number)

            def make_scores(t, k):
                s = t.s
                u, stage, b = t.unit(s.steps.index(k))
                if b == 0:
                    for i in range(KC):
                        bank, number = t.bank(("Q", stage, i), earlier=(stage == "C"))
                        pe.wait_ge(drained[bank], number)
                if b % 2 == 0:
                    pe.wait_ge(blocks_loaded[stage][b // 2], (t.group(s.steps.index(k)) + 1) * HC * 16)
                for c in range(KC):
                    wait(pe, masked_made, u * H - H + HC * (c + 1))
                    moving = lambda j: key_blocks[:, c, j, :, b * P:(b + 1) * P]
                    stationary = lambda i: queries[stage][:, i, c, b * P:(b + 1) * P]
                    three_passes(p_scores[:, c, :].rearrange("p (h n) -> p h n", h=HC), [(stationary, moving)]
                                 ).then_inc(scores_made, 1)

            def lagging(t, op, r):
                u, stage, b = t.unit(r)
                par = (r if r >= 0 else r + 8) % 2
                if op == "T":
                    for c in range(KC):
                        pe.wait_ge(probs_made, u * KC + c + 1)
                        wait(pe, turned_out0 if c == 0 else turned_out1, u)
                        for h in range(HC):
                            last = nc.tensor.transpose(p_probs[:, c, h * P:(h + 1) * P], scores[:, par, HC * c + h, :],
                                                       ident[:, :])
                        last.then_inc(probs_turned, 1)
                if op == "V":
                    bank, dst = take(t, ("O", r))
                    pe.wait_ge(turned_out0, u + 1)
                    pe.wait_ge(turned_out1, u + 1)
                    if b == 0:
                        for i in range(2):
                            bv_, nv_ = t.bank(("V", stage, i), earlier=(stage == "C"))
                            pe.wait_ge(drained[bv_], nv_)
                    for h in range(H):
                        j, c = h % HC, h // HC
                        last = nc.tensor.matmul(dst[HD * j:HD * (j + 1), c * P:(c + 1) * P],
                                                values[stage][:, b, h * HD:(h + 1) * HD], probs_t[:, h, :],
                                                start=True, stop=True)
                    last.then_inc(filled[bank], 1)
                if op == "W":
                    bank, number = t.bank(("O", r))
                    pe.wait_ge(drained[bank], number)
                    bank, dst = take(t, ("W", r))
                    w = weight[weights_of[stage][3]]
                    three_passes(dst[:, 0:D], [(lambda i, c=c: heads_t[:, i, c, :], lambda j, c=c: w[:, j, c, :])
                                               for c in range(KC)]
                                 ).then_inc(filled[bank], 1)

            def body(t):
                s = t.s
                setup_over(pe, t)
                for k in range(STEPS):
                    lag = s.lag.get(k, [])
                    for op in s.first.get(k, []):
                        work(t, op)
                    if k in s.units:
                        make_scores(t, k)
                    for op, r in only("V", lag):
                        lagging(t, op, r)
                    for op in s.early.get(k, []):
                        work(t, op)
                    for op, r in only("T", lag):
                        lagging(t, op, r)
                    for op in s.mid.get(k, []):
                        work(t, op)
                    for op, r in only("W", lag):
                        lagging(t, op, r)
                    for op in s.fill.get(k, []):
                        work(t, op)
                    for op, r in s.tail if k == s.steps[-1] else []:
                        lagging(t, op, r)

            run_pipeline(pe, shapes, body)


WEIGHTS = (["L0_gnn_" + n for n in ("ln1_g", "ln1_b", "ln2_g", "ln2_b", "wq", "bq", "wk", "bk", "wv", "bv",
                                    "wo", "bo", "w1", "b1", "w2", "b2")]
           + ["L1_gnn_" + n for n in ("Wq", "bq", "Wk", "bk", "Wv", "bv", "Wo", "bo", "gamma", "beta")])


def kernel(**inputs):
    import concourse.bacc as bacc
    from concourse.bass_utils import run_bass_kernel_spmd

    nc = bacc.Bacc("TRN2", target_bir_lowering=False, num_devices=1)
    arrays, tensors = {}, {}
    for name in ["x", "adj"] + WEIGHTS:
        a = np.ascontiguousarray(inputs[name])
        arrays["in_" + name] = a
        tensors[name] = nc.dram_tensor("in_" + name, a.shape, mybir.dt.from_np(a.dtype), kind="ExternalInput").ap()
    out = nc.dram_tensor("out", (B, P, D), F32, kind="ExternalOutput").ap()
    build(nc, tensors, out)
    results = run_bass_kernel_spmd(nc, [arrays], core_ids=[0])
    return results.results[0]["out"]
```
